# Optimizing a Trainium2 kernel written in Bass

```python
import numpy as np
import jax
import jax.numpy as jnp

def _softmax(x, axis=-1):
    return jax.nn.softmax(x, axis=axis)

def _gelu(x):
    return jax.nn.gelu(x, approximate=True)

def _silu(x):
    return jax.nn.silu(x)

def _sigmoid(x):
    return jax.nn.sigmoid(x)

def _layernorm(x, axis=-1, eps=1e-05):
    m = jnp.mean(x, axis=axis, keepdims=True)
    v = jnp.var(x, axis=axis, keepdims=True)
    return (x - m) / jnp.sqrt(v + eps)

def _scatter_add(tgt, idx, src, axis=0):
    return tgt.at[idx].add(src)

def _segment_sum(src, seg, n):
    return jax.ops.segment_sum(src, seg, n)
kernel_name = 'mk_seq_postln_d1_jaxref_r8_d602ba'

def setup_inputs(seed: int=0):
    np.random.seed(seed)
    _w = jnp.asarray

    def _L0_attn_setup():
        import jax, jax.numpy as jnp
        import numpy as np
        DIM = 128
        N_HEADS = 16
        B, T = (2, 256)
        key = jax.random.key(seed)
        ks = jax.random.split(key, 9)
        s = 1.0 / np.sqrt(DIM)
        return {'x': jax.random.normal(ks[0], (B, T, DIM), dtype=jnp.float32), 'Wq': jax.random.normal(ks[1], (DIM, DIM), dtype=jnp.float32) * s, 'bq': jnp.zeros((DIM,), dtype=jnp.float32), 'Wk': jax.random.normal(ks[2], (DIM, DIM), dtype=jnp.float32) * s, 'bk': jnp.zeros((DIM,), dtype=jnp.float32), 'Wv': jax.random.normal(ks[3], (DIM, DIM), dtype=jnp.float32) * s, 'bv': jnp.zeros((DIM,), dtype=jnp.float32), 'Wo': jax.random.normal(ks[4], (DIM, DIM), dtype=jnp.float32) * s, 'bo': jnp.zeros((DIM,), dtype=jnp.float32)}
    _L0_attn_in = _L0_attn_setup()

    def _L0_ffn_setup():
        import jax, jax.numpy as jnp
        import numpy as np
        B, S, D, E, F = (2, 128, 128, 14, 256)
        key = jax.random.key(seed)
        k0, k1, k2, k3 = jax.random.split(key, 4)
        h = jax.random.normal(k0, (B, S, D), jnp.float32)
        gate_w = jax.random.normal(k1, (E, D), jnp.float32) * 0.02
        w1 = jax.random.normal(k2, (E, D, F), jnp.float32) * (1.0 / np.sqrt(D).astype(np.float32))
        b1 = jnp.zeros((E, F), jnp.float32)
        w2 = jax.random.normal(k3, (E, F, D), jnp.float32) * (1.0 / np.sqrt(F).astype(np.float32))
        b2 = jnp.zeros((E, D), jnp.float32)
        return {'h': h, 'gate_w': gate_w, 'w1': w1, 'b1': b1, 'w2': w2, 'b2': b2}
    _L0_ffn_in = _L0_ffn_setup()
    _d = {'L0_attn_x': _L0_attn_in['x'], 'L0_attn_Wq': _L0_attn_in['Wq'], 'L0_attn_bq': _L0_attn_in['bq'], 'L0_attn_Wk': _L0_attn_in['Wk'], 'L0_attn_bk': _L0_attn_in['bk'], 'L0_attn_Wv': _L0_attn_in['Wv'], 'L0_attn_bv': _L0_attn_in['bv'], 'L0_attn_Wo': _L0_attn_in['Wo'], 'L0_attn_bo': _L0_attn_in['bo'], 'L0_ffn_gate_w': _L0_ffn_in['gate_w'], 'L0_ffn_w1': _L0_ffn_in['w1'], 'L0_ffn_b1': _L0_ffn_in['b1'], 'L0_ffn_w2': _L0_ffn_in['w2'], 'L0_ffn_b2': _L0_ffn_in['b2']}
    _x0 = _d['L0_attn_x']
    _d['L0_attn_x'] = jax.random.normal(jax.random.fold_in(jax.random.key(seed), 1), (8, 512, 128), dtype=_x0.dtype)
    del _x0
    return _d

def reference(L0_attn_x, L0_attn_Wq, L0_attn_bq, L0_attn_Wk, L0_attn_bk, L0_attn_Wv, L0_attn_bv, L0_attn_Wo, L0_attn_bo, L0_ffn_gate_w, L0_ffn_w1, L0_ffn_b1, L0_ffn_w2, L0_ffn_b2):

    def _L0_attn_ref(x, Wq, bq, Wk, bk, Wv, bv, Wo, bo):
        import jax, jax.numpy as jnp
        import numpy as np
        DIM = 128
        N_HEADS = 16
        B, T = (2, 256)
        Bv, Tv, d = x.shape
        n = N_HEADS
        hd = d // n
        Q = x @ Wq.T + bq
        K = x @ Wk.T + bk
        V = x @ Wv.T + bv
        Q = Q.reshape(Bv, Tv, n, hd).transpose(0, 2, 1, 3)
        K = K.reshape(Bv, Tv, n, hd).transpose(0, 2, 1, 3)
        V = V.reshape(Bv, Tv, n, hd).transpose(0, 2, 1, 3)
        scale = 1.0 / jnp.sqrt(jnp.asarray(d, dtype=x.dtype))
        scores = jnp.einsum('bnqd,bnkd->bnqk', Q, K) * scale
        causal = jnp.tril(jnp.ones((Tv, Tv), dtype=bool))
        scores = jnp.where(causal, scores, jnp.asarray(-jnp.inf, dtype=scores.dtype))
        attn = jax.nn.softmax(scores, axis=-1)
        out = jnp.einsum('bnqk,bnkd->bnqd', attn, V)
        out = out.transpose(0, 2, 1, 3).reshape(Bv, Tv, d)
        return out @ Wo.T + bo

    def _L0_ffn_ref(h, gate_w, w1, b1, w2, b2):
        import jax, jax.numpy as jnp
        import numpy as np
        B, S, D, E, F = (2, 128, 128, 14, 256)
        Bb, Ss, Dd = h.shape
        x = h.reshape(Bb * Ss, Dd)
        logits = x @ gate_w.T
        probs = jax.nn.softmax(logits, axis=-1)
        top2_p, top2_i = jax.lax.top_k(probs, 2)
        w = top2_p / jnp.maximum(top2_p.sum(-1, keepdims=True), 1e-10)
        hh = jnp.einsum('nd,edf->nef', x, w1) + b1
        hh = jax.nn.gelu(hh, approximate=False)
        all_out = jnp.einsum('nef,efd->ned', hh, w2) + b2
        n = jnp.arange(x.shape[0])
        out0 = all_out[n, top2_i[:, 0]]
        out1 = all_out[n, top2_i[:, 1]]
        moe_out = w[:, 0:1] * out0 + w[:, 1:2] * out1
        result = jnp.clip(x + moe_out, -100.0, 100.0).reshape(Bb, Ss, Dd)
        return result
    x = L0_attn_x
    x = _layernorm(x + _L0_attn_ref(x, L0_attn_Wq, L0_attn_bq, L0_attn_Wk, L0_attn_bk, L0_attn_Wv, L0_attn_bv, L0_attn_Wo, L0_attn_bo), axis=-1)
    x = _layernorm(x + _L0_ffn_ref(x, L0_ffn_gate_w, L0_ffn_w1, L0_ffn_b1, L0_ffn_w2, L0_ffn_b2), axis=-1)
    return x

_drawn_inputs = setup_inputs


def setup_inputs(seed=0):
    import zlib

    import numpy as np

    out = dict(_drawn_inputs(seed))
    spreads = {'L0_attn_bq': (0.0, 0.63),
     'L0_attn_bk': (0.0, 0.8),
     'L0_attn_bv': (0.0, 0.1),
     'L0_attn_bo': (0.0, 0.1),
     'L0_ffn_b1': (0.0, 0.348),
     'L0_ffn_b2': (0.0, 0.1)}
    factors = {}
    for name, (base, spread) in spreads.items():
        noise = np.random.default_rng([zlib.crc32(name.encode()), seed]).standard_normal(out[name].shape)
        drawn = base * np.exp(spread * noise) if base else spread * noise
        out[name] = jnp.asarray(drawn.astype(out[name].dtype))
    for name, factor in factors.items():
        out[name] = (out[name] * factor).astype(out[name].dtype)
    return out
```

```python
from contextlib import ExitStack

import concourse.bass as bass
from concourse import mybir

ALU = mybir.AluOpType
ACT = mybir.ActivationFunctionType
AX = mybir.AxisListType
F32 = mybir.dt.float32
F32R = mybir.dt.float32r
BF16 = mybir.dt.bfloat16
I32 = mybir.dt.int32


def post_ln_attention_moe(nc, x, xT, WqT, bq, WkT, bk, WvT, bv, WoT, bo, gateT, w1, b1, w2, b2, out):
    B, T, D = x.shape
    P = 128
    H = 16
    HD = D // H
    NQ = T // P
    NG = H // 4
    E, _, F = w1.shape
    FC = F // P
    NTOK = B * T
    TILES = NTOK // P
    TOPK = 2
    REG = NTOK + P
    ROW = D + 4
    DUMP = E * REG
    STEP = 6
    NT = -(-(NTOK * TOPK // P + E - 1) // STEP) * STEP
    SCALE = 1.0 / float(D) ** 0.5
    EPS = 1e-5
    NEG = -1e30
    NBANK = 10
    NUNIT = 6
    EB = NQ * E

    with ExitStack() as ctx:
        def sb(name, shape, dt=F32):
            return ctx.enter_context(nc.sbuf_tensor(name, shape, dt))

        def sem(name):
            return ctx.enter_context(nc.semaphore(name))

        dq = nc.dram_tensor("dq", [H, 4, HD, T], F32).ap()
        dk = nc.dram_tensor("dk", [H, 4, HD, T], F32).ap()
        xs_dram = nc.dram_tensor("xs_dram", [DUMP + P, ROW], F32).ap()
        o_dram = nc.dram_tensor("o_dram", [TOPK * NTOK, D], F32).ap()

        ident = sb("ident", [P, P])
        identb = sb("identb", [P, P], BF16)
        cmask = sb("cmask", [P, P], BF16)
        tri = sb("tri", [P, P], BF16)
        ones = sb("ones", [P, P], BF16)
        wq_sb, wk_sb, wv_sb, wo_sb = (sb(n, [P, P]) for n in ("wq_sb", "wk_sb", "wv_sb", "wo_sb"))
        gate_sb = sb("gate_sb", [P, E])
        bq_sb, bk_sb, bv_sb = (sb(n, [P, 1]) for n in ("bq_sb", "bk_sb", "bv_sb"))
        bo_bc = sb("bo_bc", [P, D])
        w1_sb = sb("w1_sb", [P, E * F])
        w2_sb = sb("w2_sb", [P, E * F])
        b1_parts = sb("b1_parts", [P, E * F], BF16)
        b2_parts = sb("b2_parts", [P, E * D], BF16)
        b1_sb = sb("b1_sb", [E, F])
        b2_sb = sb("b2_sb", [E, D])
        b1_third = sb("b1_third", [E, 3, F], BF16)
        b2_third = sb("b2_third", [E, 3, D], BF16)
        xT_sb = sb("xT_sb", [P, T])
        xTv_sb = sb("xTv_sb", [P, T])
        nat = {n: sb(n, [P, T], F32R) for n in ("q_hi", "q_lo", "k_hi", "k_lo")}
        qst = sb("qst", [P, NG, T], F32R)
        kst = sb("kst", [P, NG, 4, T], F32R)
        vst = sb("vst", [P, NQ, H, 32])
        nmax = sb("nmax", [P, NG, 16])
        nmrow = sb("nmrow", [16, 2, P], F32R)
        probs = sb("probs", [P, 2, 2, 5 * T])
        oT_sb = sb("oT_sb", [P, T])
        rz = sb("rz", [P, NQ * 4])
        o_sb = sb("o_sb", [P, T])
        onT_sb = sb("onT_sb", [P, T])
        xb = sb("xb", [P, NQ, D])
        xbo = sb("xbo", [P, NQ, D])
        y = sb("y", [P, NQ, D])
        st = sb("st", [P, NQ, 6])
        mv = sb("mv", [P, NQ, 2])
        rstd = sb("rstd", [P, NQ])
        vpe = sb("vpe", [P, NQ])
        mhalf = sb("mhalf", [P, NQ])
        x1 = [sb("x1_first", [P, NQ, ROW]), sb("x1_second", [P, NQ, ROW])]
        x1T_sb = sb("x1T_sb", [P, T])
        xr = sb("xr", [P, TILES * D])
        rev = sb("rev", [P, NQ, E])
        lg = sb("lg", [P, NQ, E])
        lg2 = sb("lg2", [P, NQ, E])
        tmp = sb("tmp", [P, NQ, E])
        tm1 = sb("tm1", [P, NQ, E])
        top = sb("top", [P, 4, NQ])
        hot = [sb("hot_first", [P, NQ, E]), sb("hot_second", [P, NQ, E])]
        hotb = sb("hotb", [P, NQ, E], BF16)
        rank = sb("rank", [P, NQ, E])
        nxt = sb("nxt", [P, E])
        reg0 = sb("reg0", [P, E])
        posf = sb("posf", [P, TOPK, NQ])
        pos = sb("pos", [P, TOPK, NQ], I32)
        slot = sb("slot", [P, TOPK, NQ])
        lgm = sb("lgm", [P, TILES * E])
        dm = sb("dm", [P, TILES])
        nrow = sb("nrow", [1, 6, E])
        nrow_i = sb("nrow_i", [1, 2, E], I32)
        tile_no = sb("tile_no", [1, NT])
        tile_le = sb("tile_le", [1, NT, E])
        tile_rg = sb("tile_rg", [1, NT, E])
        tile_ef = sb("tile_ef", [1, 2, NT])
        tile_ei = sb("tile_ei", [1, 2, NT], I32)
        pad = sb("pad", [P, ROW])
        gw = sb("gw", [P, 6, TILES])
        xs = sb("xs", [P, STEP, ROW])
        xsT = sb("xsT", [P, 2, P])
        h_sb = sb("h_sb", [P, 2, F])
        hT_sb = sb("hT_sb", [P, 2, F])
        y_sb = sb("y_sb", [P, 3, D])

        psum = ctx.enter_context(nc.psum_tensor("psum", [P, 8, T], F32))
        ps_s = psum[:, 0:4, :].rearrange("p (s k) t -> p s k t", s=2)
        ps_t = psum[:, 4:6, :]
        ps_o = psum[:, 6, :]
        ps_m = psum[:, 7, :]

        S = {n: sem(n) for n in """
            pool_turn dve_turn sp_turn const_loaded weights_loaded bias_loaded bias_split bias_third bias_placed
            idents_ready masks_ready iota_ready const_ready kst_zeroed scratch_src scratch_set one_row
            xT_loaded xTv_loaded x_loaded xbo_ready
            q_hi_done k_hi_done qk_stored
            m_rows st_filled exp_done s_filled s_reduced masked
            pv_filled oT_copied rz_ready
            stats_ready aggr_ready vpe_ready rstd_ready x1_ready x1_ids x1b_ready xr_copied
            top_link hot_ready rank_link pos_ready scattered
            gate_exp tab_link tables_ready padded gate_link gates_ready
            xsT_filled xsT_copied h_filled gelu_done hT_filled hT_copied y_filled y_copied
            comb_link comb_stats fin_vpe fin_rstd fin_ready out_stored
            """.split()}
        ITEMS = ("m", "ot", "q", "k", "v", "on", "wo", "x1t", "lg", "rk")
        filled = {n: sem(n + "_filled") for n in ITEMS}
        drained = {n: sem(n + "_drained") for n in ITEMS}
        xs_loaded = [sem(f"xs_loaded_{r}") for r in range(STEP)]
        y_scattered = [sem(f"y_scattered_{r}") for r in range(3)]
        o_loaded = [sem(f"o_loaded_{u}") for u in range(2)]
        qk_loaded = [sem(f"qk_loaded_{c}") for c in range(NG)]

        MISC = {(c, 1): "m" for c in range(NG)} | {(c, 8): "ot" for c in range(NG)} | {
            (0, 2): "q", (0, 4): "k", (0, 7): "v", (1, 3): "on", (1, 6): "wo", (2, 4): "x1t", (2, 6): "lg", (3, 5): "rk"}
        UNIT_AT = {0: 0, 2: 1, 3: 2, 5: 3, 7: 4, 8: 5}
        PV_AT = 5

        def live(b):
            return not isinstance(b, int) or 0 <= b < B

        def ahead(b, c, n):
            return b + (c + n) // NG, (c + n) % NG

        def owner(b, c, item):
            if item == "m":
                bb, cc = ahead(b, c, 1)
                return bb, cc, bb * NG + cc
            if item == "ot":
                bb, cc = ahead(b, c, -1)
                return bb, cc, bb * NG + cc
            bb = b + {"q": 1, "k": 1, "v": 0}.get(item, -1)
            return bb, None, bb

        ORDER = sorted(MISC)

        def before(b, c, k):
            n = ORDER.index((c, k))
            bb = b
            for _ in range(2 * len(ORDER)):
                n -= 1
                if n < 0:
                    n, bb = len(ORDER) - 1, bb - 1
                item = MISC[ORDER[n]]
                ob, _, count = owner(bb, ORDER[n][0], item)
                if live(ob):
                    return item, count + 1
            return None

        def batches(eng, body):
            body(-1)
            body(0)
            with eng.Fori(1, B - 2) as b:
                body(b)
            body(B - 2)
            body(B - 1)
            body(B)

        def expert_steps(eng, step):
            for r in range(STEP):
                step(0, r)
            with eng.Fori(1, NT // STEP) as i:
                for r in range(STEP):
                    step(i, r)
            for r in range(3):
                step(NT // STEP, r)

        def lagged(i, r, lag):
            ii = i - 1 if r < lag else i
            rr = (r - lag) % STEP
            return ii * STEP + rr, rr, ii

        def tile_live(j):
            return not isinstance(j, int) or 0 <= j < NT

        def seg(g, j):
            h = g % 2
            at = {0: h * T, 1: 2 * T + h * T, 3: 2 * T + h * T + 3 * P, 2: 4 * T + h * 2 * P}[j]
            return at, T - P * j

        block = ctx.enter_context(nc.Block())

        @block.sync
        def _(sp):
            def hold(s, n):
                sp.wait_ge(s, n)
                if not isinstance(n, int):
                    sp.sem_inc(S["sp_turn"], 1)

            for dst, src in ((wq_sb, WqT), (wk_sb, WkT), (bq_sb, bq), (bk_sb, bk)):
                sp.dma_start(dst[:], src).then_inc(S["const_loaded"], 16)
            sp.dma_start(xT_sb[:], xT[0]).then_inc(S["xT_loaded"], 16)
            sp.dma_start(xTv_sb[:], xT[0]).then_inc(S["xTv_loaded"], 16)
            for dst, src in ((wv_sb, WvT), (wo_sb, WoT), (bv_sb, bv), (gate_sb, gateT)):
                sp.dma_start(dst[:], src).then_inc(S["weights_loaded"], 16)
            sp.dma_start(bo_bc[:], bo.to_broadcast([P, D])).then_inc(S["weights_loaded"], 16)
            sp.dma_start(b1_sb[:], b1).then_inc(S["bias_loaded"], 16)
            sp.dma_start(b2_sb[:], b2).then_inc(S["bias_loaded"], 16)
            sp.wait_ge(S["scratch_src"], 2)
            zeros = probs[0:H, 0].rearrange("p a t -> p (a t)")
            for dst, src in ((dq[:, 3], zeros[:, 0:HD * T]), (dk[:, 3, 1:HD], zeros[:, 0:(HD - 1) * T]),
                             (dk[:, 3, 0:1], probs[0:H, 1, 0, 0:T])):
                sp.dma_start(dst.rearrange("h d t -> h (d t)"), src).then_inc(S["scratch_set"], 16)
            sp.dma_start(w1_sb[:].rearrange("p (e f) -> p e f", e=E), w1.rearrange("e d f -> d e f")).then_inc(S["weights_loaded"], 16)
            for ch in range(FC):
                sp.dma_start(w2_sb[:].rearrange("p (e c d) -> p e c d", e=E, c=FC)[:, :, ch, :],
                             w2.rearrange("e (c p) d -> c p e d", c=FC)[ch]).then_inc(S["weights_loaded"], 16)

            def load_stacks(b, c):
                if not (isinstance(b, int) and b == 0):
                    hold(S["st_filled"], (b - 1) * NBANK * NG + (c + 1) * NBANK)
                hold(S["qk_stored"], (b + 1) * 96)
                sp.dma_start(qst[:, c, :].bitcast(F32), dq.rearrange("(g c) r d t -> c g (r d) t", c=NG)[c]).then_inc(qk_loaded[c], 16)
                for g in range(4):
                    sp.dma_start(kst[32 * g:32 * g + 32, c, g, :].bitcast(F32),
                                 dk[NG * g + c].rearrange("r d t -> (r d) t")).then_inc(qk_loaded[c], 16)

            def body(b):
                for c in range(NG):
                    nb, ncg = ahead(b, c, 3)
                    if live(nb):
                        if isinstance(nb, int) and nb == 0 and ncg == 0:
                            sp.wait_ge(S["scratch_set"], 16 * 3)
                            sp.wait_ge(S["kst_zeroed"], 2)
                        load_stacks(nb, ncg)
                    if isinstance(b, int) and b == 0 and c == 1:
                        sp.wait_ge(S["bias_split"], 10)
                        sp.wait_ge(S["bias_third"], 1)
                        sp.wait_ge(S["const_ready"], 5)
                        for parts, third in ((b1_parts, b1_third), (b2_parts, b2_third)):
                            for r in range(3):
                                sp.dma_start(parts[r:r + 1, :].rearrange("r (e f) -> r e f", e=E),
                                             third[:, r, :]).then_inc(S["bias_placed"], 16)
                    for k in range(NBANK):
                        item = MISC.get((c, k))
                        if item == "m":
                            ob, oc, n = owner(b, c, "m")
                            if live(ob):
                                hold(drained["m"], n + 1)
                                sp.dma_start(qst[24:P:32, oc, :].bitcast(F32).rearrange("g (i q) -> g i q", i=NQ),
                                             nmrow[:, oc % 2, :].bitcast(F32)
                                             ).then_inc(S["m_rows"], 16)
                    if c == 0 and live(b + 1):
                        if not (isinstance(b, int) and b < 0):
                            for cc in range(NG):
                                hold(qk_loaded[cc], (b + 1) * 80)
                        for name, d, hi_done in (("q", dq, "q_hi_done"), ("k", dk, "k_hi_done")):
                            hold(S[hi_done], b + 2)
                            hi_parts, lo_part = ((0, 1), 2) if name == "q" else ((0, 2), 1)
                            for r in hi_parts:
                                sp.dma_start(d[:, r],
                                             nat[name + "_hi"][:].bitcast(F32)).then_inc(S["qk_stored"], 16)
                            hold(drained[name], b + 2)
                            sp.dma_start(d[:, lo_part],
                                         nat[name + "_lo"][:].bitcast(F32)).then_inc(S["qk_stored"], 16)
                        if live(b + 2):
                            hold(filled["k"], b + 2)
                            sp.dma_start(xT_sb[:], xT[bass.ds(b + 2, 1)].rearrange("b d t -> (b d) t")).then_inc(S["xT_loaded"], 16)
                    if c == 1 and live(b) and live(b + 1):
                        hold(filled["v"], b + 1)
                        sp.dma_start(xTv_sb[:], xT[bass.ds(b + 1, 1)].rearrange("b d t -> (b d) t")).then_inc(S["xTv_loaded"], 16)
                    if c == 2 and live(b):
                        if not (isinstance(b, int) and b == 0):
                            hold(S["xbo_ready"], b)
                        sp.dma_start(xb[:], x[bass.ds(b, 1)].rearrange("b (i p) d -> p (b i) d", p=P)).then_inc(S["x_loaded"], 16)
                    if c == 2 and live(b - 1):
                        hold(S["x1_ready"], b * NQ)
                        sp.dma_start(xr[:, bass.ds((b - 1) * T, T)].rearrange("p (i d) -> p i d", i=NQ),
                                     x1[0][:, :, 0:D]).then_inc(S["xr_copied"], 16)

            batches(sp, body)

            sp.wait_ge(S["iota_ready"], 6)
            sp.dma_start(xs_dram[DUMP:DUMP + P, :], pad[:]).then_inc(S["padded"], 16)
            sp.wait_ge(S["scattered"], B * NQ * TOPK * 16)
            sp.wait_ge(S["tables_ready"], 1)
            with sp.Fori(0, E) as e:
                r = sp.value_load(nrow_i[0:1, 0, bass.ds(e, 1)], min_val=0, max_val=DUMP)
                sp.dma_start(xs_dram[bass.ds(r, P), :], pad[:]).then_inc(S["padded"], 16)
            sp.wait_ge(S["padded"], 16 * (E + 1))

            def step(i, r):
                s, _, _ = lagged(i, r, 0)
                if not tile_live(s):
                    return
                if not (isinstance(s, int) and s < STEP):
                    hold(y_scattered[r % 3], 16 * (2 * i + r // 3 - 1))
                row = sp.value_load(tile_ei[0:1, 1, bass.ds(s, 1)], min_val=0, max_val=DUMP)
                sp.dma_start(xs[:, r, :], xs_dram[bass.ds(row, P), :]).then_inc(xs_loaded[r], 16)

            expert_steps(sp, step)

            for n in range(3):
                sp.wait_ge(y_scattered[n], 16 * NT // 3)

            def load_results(q, u):
                for k in range(TOPK):
                    sp.dma_start(probs[:, u, k, 0:T].rearrange("p (i d) -> p i d", i=NQ),
                                 o_dram[bass.ds(q * T + k * NTOK, T), :].rearrange("(i p) d -> p i d", p=P)
                                 ).then_inc(o_loaded[u], 16)

            def store(q, u):
                hold(S["fin_ready"], q + 1)
                sp.dma_start(out[bass.ds(q, 1)].rearrange("b (i p) d -> p (b i) d", p=P),
                             probs[:, u, 0, 2 * T:3 * T].rearrange("p (i d) -> p i d", i=NQ)).then_inc(S["out_stored"], 16)

            load_results(0, 0)
            load_results(1, 1)
            with sp.Fori(0, B // 2 - 1) as i:
                for u in range(2):
                    store(i * 2 + u, u)
                    load_results(i * 2 + u + 2, u)
            store(B - 2, 0)
            store(B - 1, 1)
            sp.wait_ge(S["out_stored"], 16 * B)

        @block.gpsimd
        def _(pool):
            pool.memset(kst[:, 0:2].bitcast(F32), 0.0).then_inc(S["kst_zeroed"], 1)
            pool.memset(ident[:], 0.0).then_inc(S["idents_ready"], 1)
            pool.memset(identb[:], 0.0).then_inc(S["idents_ready"], 1)
            pool.memset(cmask[:], 0.0).then_inc(S["masks_ready"], 1)
            pool.memset(tri[:], 1.0).then_inc(S["masks_ready"], 1)
            pool.wait_ge(S["idents_ready"], 2)
            for m in (ident, identb):
                pool.affine_select(out=m[:], in_=m[:], compare_op=ALU.not_equal, fill=1.0, base=0,
                                   pattern=[[-1, P]], channel_multiplier=1).then_inc(S["idents_ready"], 1)
            pool.wait_ge(S["masks_ready"], 2)
            pool.affine_select(out=cmask[:], in_=cmask[:], compare_op=ALU.is_ge, fill=NEG, base=0,
                               pattern=[[-1, P]], channel_multiplier=1).then_inc(S["masks_ready"], 1)
            pool.affine_select(out=tri[:], in_=tri[:], compare_op=ALU.is_gt, fill=0.0, base=0,
                               pattern=[[1, P]], channel_multiplier=-1).then_inc(S["masks_ready"], 1)
            pool.iota(rev[:], [[0, NQ], [-1, E]], base=E, channel_multiplier=0,
                      allow_small_or_imprecise_dtypes=True).then_inc(S["iota_ready"], 1)
            pool.iota(nxt[:], [[REG, E]], base=0, channel_multiplier=0,
                      allow_small_or_imprecise_dtypes=True).then_inc(S["iota_ready"], 1)
            pool.iota(slot[:], [[NTOK, TOPK], [P, NQ]], base=0, channel_multiplier=1,
                      allow_small_or_imprecise_dtypes=True).then_inc(S["iota_ready"], 1)
            pool.iota(tile_no[:], [[1, NT]], base=0, channel_multiplier=0,
                      allow_small_or_imprecise_dtypes=True).then_inc(S["iota_ready"], 1)
            pool.memset(pad[:, 0:D], 0.0).then_inc(S["iota_ready"], 1)
            pool.iota(pad[:, D:ROW].bitcast(I32), [[0, ROW - D]], base=TOPK * NTOK,
                      channel_multiplier=1).then_inc(S["iota_ready"], 1)
            pool.iota(reg0[:], [[REG, E]], base=0, channel_multiplier=0,
                      allow_small_or_imprecise_dtypes=True).then_inc(S["iota_ready"], 1)
            pool.memset(mhalf[:], -0.5).then_inc(S["const_ready"], 1)

            def turn():
                pool.sem_inc(S["pool_turn"], 1)

            def body(b):
                for c in range(NG):
                    if live(b):
                        n = (b * NG + c) * NBANK
                        for p in range(2):
                            pr = probs[:, c % 2, p, :]
                            for upto, view in (
                                    (4, pr[:, 0:4 * T].rearrange("p (n t) -> p n t", t=T)[:, :, 0:P]),
                                    (4, pr[:, 2 * T:4 * T].rearrange("p (n t) -> p n t", t=T)[:, :, 3 * P:4 * P]),
                                    (5, pr[:, 4 * T:5 * T].rearrange("p (n t) -> p n t", t=2 * P)[:, :, 0:P])):
                                pool.wait_ge(S["exp_done"], n + 5 * p + upto)
                                turn()
                                pool.affine_select(out=view, in_=view, compare_op=ALU.is_ge, fill=0.0, base=0,
                                                   pattern=[[0, view.shape[1]], [1, P]], channel_multiplier=-1
                                                   ).then_inc(S["masked"], 1)
                    if c == 2 and live(b):
                        pool.wait_ge(S["x_loaded"], 16 * (b + 1))
                        turn()
                        if not (isinstance(b, int) and b == 0):
                            pool.wait_ge(drained["wo"], b)
                            turn()
                        else:
                            pool.wait_ge(S["weights_loaded"], 16 * 8)
                        pool.tensor_tensor(xbo[:], xb[:], bo_bc[:].unsqueeze(1).to_broadcast([P, NQ, D]),
                                           ALU.add).then_inc(S["xbo_ready"], 1)
                    if c == 1 and live(b - 1):
                        pool.wait_ge(S["aggr_ready"], NQ * b)
                        turn()
                        pool.tensor_scalar(vpe[:], mv[:, :, 1], EPS, None, ALU.add).then_inc(S["vpe_ready"], 1)
                        pool.wait_ge(S["vpe_ready"], b)
                        turn()
                        pool.tensor_tensor(rstd[:], vpe[:], mhalf[:], ALU.pow).then_inc(S["rstd_ready"], 1)
                    if c == 3 and live(b - 1):
                        pool.wait_ge(S["pos_ready"], b)
                        turn()
                        pool.wait_ge(S["x1_ids"], b)
                        turn()
                        pool.wait_ge(S["x1b_ready"], b)
                        turn()
                        for k in range(TOPK):
                            for i in range(NQ):
                                turn()
                                pool.indirect_dma_start(
                                    xs_dram, bass.IndirectOffsetOnAxis(pos[:, k, i:i + 1], 0), x1[k][:, i, :], None,
                                    bounds_check=DUMP - 1).then_inc(S["scattered"], 16)

            batches(pool, body)

            def step(i, r):
                j, u, _ = lagged(i, r, 3)
                if not tile_live(j):
                    return
                pool.wait_ge(S["y_copied"], j + 1)
                turn()
                pool.indirect_dma_start(
                    o_dram, bass.IndirectOffsetOnAxis(xs[:, u, D:D + 1].bitcast(I32), 0), y_sb[:, u % 3, :], None,
                    bounds_check=TOPK * NTOK - 1, oob_is_err=False).then_inc(y_scattered[u % 3], 16)

            expert_steps(pool, step)
            with pool.Fori(0, B) as q:
                pool.wait_ge(S["comb_stats"], NQ * (q + 1))
                turn()
                pool.tensor_scalar(vpe[:], mv[:, :, 1], EPS, None, ALU.add).then_inc(S["fin_vpe"], 1)
                pool.wait_ge(S["fin_vpe"], q + 1)
                turn()
                pool.tensor_tensor(rstd[:], vpe[:], mhalf[:], ALU.pow).then_inc(S["fin_rstd"], 1)

        @block.scalar
        def _(act):
            def exp_bank(b, c, k):
                n = (b * NG + c) * NBANK + k
                act.wait_ge(S["st_filled"], n + 1)
                if k == 0 and not (isinstance(b, int) and b * NG + c < 2):
                    act.wait_ge(S["pv_filled"], b * NG + c - 1)
                p, kk = k // 5, k % 5
                act.activation(probs[:, c % 2, p, kk * T:(kk + 1) * T], ps_t[:, k % 2, :], ACT.Exp,
                               scale=SCALE).then_inc(S["exp_done"], 1)

            def split_hi(b, name, bias):
                act.wait_ge(filled[name], b + 1)
                if isinstance(b, int) and b == 0:
                    act.wait_ge(S["const_loaded"], 64)
                else:
                    act.wait_ge(S["qk_stored"], b * 96)
                act.activation(nat[name + "_hi"][:], ps_m, ACT.Identity, bias=bias[:, 0:1]
                               ).then_inc(S[name + "_hi_done"], 1)

            def body(b):
                for c in range(NG):
                    for k in range(NBANK):
                        if live(b):
                            exp_bank(b, c, k)
                        item = MISC.get((c, k))
                        if k == PV_AT:
                            ob, oc = ahead(b, c, -1)
                            if live(ob):
                                n = ob * NG + oc
                                act.wait_ge(S["pv_filled"], n + 1)
                                if not (isinstance(n, int) and n == 0):
                                    act.wait_ge(filled["ot"], n)
                                act.activation(oT_sb[:], ps_o, ACT.Copy).then_inc(S["oT_copied"], 1)
                        if item is None or not live(owner(b, c, item)[0]):
                            continue
                        ob = owner(b, c, item)[0]
                        if item == "q":
                            split_hi(ob, "q", bq_sb)
                        if item == "k":
                            split_hi(ob, "k", bk_sb)
                        if item == "v":
                            act.wait_ge(filled["v"], ob + 1)
                            if isinstance(ob, int) and ob == 0:
                                act.wait_ge(S["const_ready"], 5)
                            act.activation(vst[:].rearrange("p i h w -> p (i h) w")[:, :, 0:HD],
                                           ps_m.rearrange("p (n d) -> p n d", d=HD), ACT.Copy).then_inc(drained["v"], 1)
                        if item == "on":
                            act.wait_ge(filled["on"], ob + 1)
                            if isinstance(ob, int) and ob == 0:
                                act.wait_ge(S["weights_loaded"], 16 * 8)
                            act.activation(onT_sb[:], ps_m, ACT.Identity, bias=bv_sb[:, 0:1]).then_inc(drained["on"], 1)
                        if item == "x1t":
                            act.wait_ge(S["x1_ready"], NQ * (ob + 1))
                            act.activation(x1[1][:, :, 0:D], x1[0][:, :, 0:D], ACT.Copy).then_inc(S["x1b_ready"], 1)
                            act.wait_ge(filled["x1t"], ob + 1)
                            act.activation(x1T_sb[:], ps_m, ACT.Copy).then_inc(drained["x1t"], 1)

            batches(act, body)
            act.wait_ge(S["top_link"], 15 * B)
            act.activation(lgm[:], lgm[:], ACT.Exp).then_inc(S["gate_exp"], 1)
            act.activation(dm[:], dm[:], ACT.Exp).then_inc(S["gate_exp"], 1)

            def step(i, r):
                j, u, _ = lagged(i, r, 1)
                if tile_live(j):
                    act.wait_ge(S["h_filled"], j + 1)
                    if not (isinstance(j, int) and j < 2):
                        act.wait_ge(S["hT_filled"], j - 1)
                    act.activation(h_sb[:, u % 2, :], psum[:, 2 + u % 2, 0:F], ACT.Gelu).then_inc(S["gelu_done"], 1)
                j, u, ii = lagged(i, r, 3)
                if tile_live(j):
                    act.wait_ge(S["y_filled"], j + 1)
                    if not (isinstance(j, int) and j < 3):
                        act.wait_ge(y_scattered[u % 3], 16 * (2 * ii + u // 3))
                    act.activation(y_sb[:, u % 3, :], psum[:, 6 + u % 2, 0:D], ACT.Copy).then_inc(S["y_copied"], 1)

            expert_steps(act, step)

        @block.tensor
        def _(pe):
            pe.wait_ge(S["idents_ready"], 4)
            pe.wait_ge(S["masks_ready"], 4)
            pe.wait_ge(S["const_ready"], 5)

            def score_unit(b, c, u):
                n = (b * NG + c) * NUNIT + u
                if u == 0:
                    pe.wait_ge(qk_loaded[c], 80 * (b + 1))
                if not (isinstance(n, int) and n < 2):
                    pe.wait_ge(S["s_reduced"], n - 1)
                pair, kind = u // 3, u % 3
                for h in range(2):
                    g = 2 * pair + h
                    parts = {0: [(3, h, 0)], 1: [(2, h, 0), (0, h, 3 * P)], 2: [(1, 0, 2 * P * h)]}[kind]
                    for i, bank, at in parts:
                        w = P * (i + 1)
                        o = ps_s[:, u % 2, bank, :]
                        pe.matmul(o[:, at:at + w], qst[:, c, P * i:P * i + P], kst[:, c, g, 0:w], start=True, stop=False)
                        last = pe.matmul(o[:, at + w - P:at + w], identb[:], cmask[:], start=False, stop=True)
                last.then_inc(S["s_filled"], 1)

            def score_bank(b, c, k):
                n = (b * NG + c) * NBANK + k
                if k == 0:
                    pe.wait_ge(S["m_rows"], 16 * (b * NG + c + 1))
                if not (isinstance(n, int) and n < 2):
                    pe.wait_ge(S["exp_done"], n - 1)
                pair, kk = k // 5, k % 5
                for g in (2 * pair, 2 * pair + 1):
                    for j in range(NQ):
                        at, w = seg(g, j)
                        if at // T == kk:
                            last = pe.matmul(ps_t[:, k % 2, at % T:at % T + w], kst[:, c, g, P * j:P * j + P],
                                             qst[:, c, P * j:T], start=True, stop=True)
                last.then_inc(S["st_filled"], 1)

            def pv(b, c):
                n = b * NG + c
                pe.wait_ge(S["masked"], 6 * (n + 1))
                pe.wait_ge(drained["v"], b + 1)
                if not (isinstance(n, int) and n == 0):
                    pe.wait_ge(S["oT_copied"], n)
                for j in range(NQ):
                    for g in range(4):
                        at, w = seg(g, j)
                        last = pe.matmul(ps_o[32 * g:32 * g + 32, P * j:T], vst[:, j, 4 * g + c, :],
                                         probs[:, c % 2, g // 2, at:at + w], start=(j == 0), stop=(j == NQ - 1))
                last.then_inc(S["pv_filled"], 1)

            def shared(b, c, k, item):
                ob, oc, n = owner(b, c, item)
                if not live(ob):
                    return
                prev = before(b, c, k)
                if prev is not None:
                    pe.wait_ge(drained[prev[0]], prev[1])
                if item == "m":
                    pe.wait_ge(S["s_reduced"], NUNIT * (n + 1))
                    last = pe.transpose(ps_m[0:16, 0:P], nmax[:, oc, :], ident[:])
                if item == "ot":
                    pe.wait_ge(S["oT_copied"], n + 1)
                    for i in range(NQ):
                        last = pe.transpose(ps_m[:, P * i:P * i + P], oT_sb[:, P * i:P * i + P], ident[:])
                if item in ("q", "k"):
                    if isinstance(ob, int) and ob == 0:
                        pe.wait_ge(S["const_loaded"], 64)
                    pe.wait_ge(S["xT_loaded"], 16 * (ob + 1))
                    last = pe.matmul(ps_m, (wq_sb if item == "q" else wk_sb)[:], xT_sb[:], start=True, stop=True)
                if item == "v":
                    if isinstance(ob, int) and ob == 0:
                        pe.wait_ge(S["weights_loaded"], 16 * 8)
                    pe.wait_ge(S["xTv_loaded"], 16 * (ob + 1))
                    for i in range(NQ):
                        last = pe.matmul(ps_m[:, P * i:P * i + P], xTv_sb[:, P * i:P * i + P], wv_sb[:],
                                         start=True, stop=True)
                if item == "on":
                    pe.wait_ge(drained["ot"], NG * (ob + 1))
                    for i in range(NQ):
                        last = pe.transpose(ps_m[:, P * i:P * i + P], o_sb[:, P * i:P * i + P], ident[:])
                if item == "wo":
                    pe.wait_ge(drained["on"], ob + 1)
                    for i in range(NQ):
                        last = pe.matmul(ps_m[:, P * i:P * i + P], onT_sb[:, P * i:P * i + P], wo_sb[:],
                                         start=True, stop=True)
                if item == "x1t":
                    pe.wait_ge(S["x1_ready"], NQ * (ob + 1))
                    for i in range(NQ):
                        last = pe.transpose(ps_m[:, P * i:P * i + P], x1[0][:, i, 0:D], ident[:])
                if item == "lg":
                    pe.wait_ge(drained["x1t"], ob + 1)
                    for i in range(NQ):
                        last = pe.matmul(ps_m[:, E * i:E * i + E], x1T_sb[:, P * i:P * i + P], gate_sb[:],
                                         start=True, stop=True)
                if item == "rk":
                    pe.wait_ge(S["hot_ready"], ob + 1)
                    pe.matmul(ps_m[:, 0:EB], tri[:], hotb[:].rearrange("p i e -> p (i e)"), start=True, stop=False,
                              skip_group_check=True)
                    for i in range(NQ):
                        for o in range(i + 1, NQ):
                            pe.matmul(ps_m[:, E * o:E * o + E], ones[:], hotb[:, i, :], start=False, stop=False,
                                      skip_group_check=True)
                        last = pe.matmul(ps_m[:, EB:EB + E], ones[:], hotb[:, i, :], start=False, stop=(i == NQ - 1),
                                         skip_group_check=True)
                last.then_inc(filled[item], 1)

            def body(b):
                for c in range(NG):
                    sb_, sc_ = ahead(b, c, 2)
                    pb_, pc_ = ahead(b, c, -1)
                    for k in range(NBANK):
                        if live(b):
                            score_bank(b, c, k)
                        if k in UNIT_AT and live(sb_):
                            score_unit(sb_, sc_, UNIT_AT[k])
                        if k == PV_AT and live(pb_):
                            pv(pb_, pc_)
                        if (c, k) in MISC:
                            shared(b, c, k, MISC[(c, k)])

            batches(pe, body)
            pe.wait_ge(drained["rk"], B)
            pe.wait_ge(S["weights_loaded"], 16 * 8)
            pe.wait_ge(S["bias_placed"], 16 * 6)
            pe.wait_ge(S["tables_ready"], 1)

            def step(i, r):
                j, u, ii = lagged(i, r, 0)
                if tile_live(j):
                    pe.wait_ge(xs_loaded[r], 16 * (ii + 1))
                    if not (isinstance(j, int) and j < 2):
                        pe.wait_ge(S["xsT_copied"], j - 1)
                    pe.transpose(psum[:, r % 2, 0:P], xs[:, r, 0:D], ident[:]).then_inc(S["xsT_filled"], 1)
                j, u, ii = lagged(i, r, 1)
                if tile_live(j):
                    e = pe.value_load(tile_ei[0:1, 0, bass.ds(j, 1)], min_val=0, max_val=E - 1)
                    pe.wait_ge(S["xsT_copied"], j + 1)
                    if not (isinstance(j, int) and j < 2):
                        pe.wait_ge(S["gelu_done"], j - 1)
                    pe.matmul(psum[:, 2 + u % 2, 0:F], xsT[:, u % 2, :], w1_sb[:, bass.ds(e * F, F)], start=True, stop=False)
                    pe.matmul(psum[:, 2 + u % 2, 0:F], ones[:], b1_parts[:, bass.ds(e * F, F)], start=False, stop=True
                              ).then_inc(S["h_filled"], 1)
                j, u, ii = lagged(i, r, 2)
                if tile_live(j):
                    pe.wait_ge(S["gelu_done"], j + 1)
                    if not (isinstance(j, int) and j < 2):
                        pe.wait_ge(S["hT_copied"], j - 1)
                    for ch in range(FC):
                        last = pe.transpose(psum[:, 4 + u % 2, P * ch:P * ch + P], h_sb[:, u % 2, P * ch:P * ch + P], ident[:])
                    last.then_inc(S["hT_filled"], 1)
                j, u, ii = lagged(i, r, 3)
                if tile_live(j):
                    e = pe.value_load(tile_ei[0:1, 0, bass.ds(j, 1)], min_val=0, max_val=E - 1)
                    pe.wait_ge(S["hT_copied"], j + 1)
                    if not (isinstance(j, int) and j < 2):
                        pe.wait_ge(S["y_copied"], j - 1)
                    for ch in range(FC):
                        pe.matmul(psum[:, 6 + u % 2, 0:D], hT_sb[:, u % 2, P * ch:P * ch + P],
                                  w2_sb[:, bass.ds(e * F + P * ch, D)], start=(ch == 0), stop=False)
                    pe.matmul(psum[:, 6 + u % 2, 0:D], ones[:], b2_parts[:, bass.ds(e * D, D)], start=False, stop=True
                              ).then_inc(S["y_filled"], 1)

            expert_steps(pe, step)

        @block.vector
        def _(dve):
            def linker(s, base):
                n = [0]

                def link(ins):
                    n[0] += 1
                    ins.then_inc(s, 1)
                    dve.wait_ge(s, base + n[0])
                return link

            dve.memset(probs[0:H, 0], 0.0).then_inc(S["scratch_src"], 1)
            dve.memset(probs[0:H, 1, 0, 0:T], 1.0).then_inc(S["scratch_src"], 1)
            dve.memset(kst[:, 2:4].bitcast(F32), 0.0).then_inc(S["kst_zeroed"], 1)
            dve.memset(ones[:], 1.0).then_inc(S["const_ready"], 1)
            dve.memset(vst[:, :, :, HD + 1:32], 0.0).then_inc(S["const_ready"], 1)
            dve.memset(vst[:, :, :, HD:HD + 1], 1.0).then_inc(S["const_ready"], 1)
            dve.memset(b1_parts[:], 0.0).then_inc(S["const_ready"], 1)
            dve.memset(b2_parts[:], 0.0).then_inc(S["bias_third"], 1)
            dve.wait_ge(S["iota_ready"], 3)

            dve.wait_ge(S["bias_loaded"], 32)
            split = linker(S["bias_split"], 0)
            for b_sb, third in ((b1_sb, b1_third), (b2_sb, b2_third)):
                for r in range(3):
                    split(dve.tensor_copy(third[:, r, :], b_sb[:]))
                    if r < 2:
                        split(dve.tensor_tensor(b_sb[:], b_sb[:], third[:, r, :], ALU.subtract))

            def reduce_unit(b, c, u):
                n = (b * NG + c) * NUNIT + u
                dve.wait_ge(S["s_filled"], n + 1)
                pair, kind = u // 3, u % 3
                ps = ps_s[:, u % 2]
                mx = nmax[:, c, :].rearrange("p (g i) -> p g i", g=4)[:, 2 * pair:2 * pair + 2, :]
                if kind == 0:
                    todo = [(mx[:, :, 3], ps[:, :, :])]
                elif kind == 1:
                    todo = [(mx[:, :, 2], ps[:, :, 0:3 * P]), (mx[:, :, 0], ps[:, :, 3 * P:T])]
                else:
                    todo = [(mx[:, :, 1], ps[:, 0, :].rearrange("p (h w) -> p h w", h=2))]
                for o, i in todo:
                    last = dve.tensor_reduce(o, i, AX.X, ALU.max, negate=True)
                last.then_inc(S["s_reduced"], 1)

            def shared(b, c, item):
                ob, oc, n = owner(b, c, item)
                if not live(ob):
                    return
                first = isinstance(ob, int) and ob == 0
                done = drained[item]
                if item == "m":
                    dve.wait_ge(filled["m"], n + 1)
                    if not (isinstance(n, int) and n < 2):
                        dve.wait_ge(S["m_rows"], 16 * (n - 1))
                    dve.tensor_copy(nmrow[:, oc % 2, :], ps_m[0:16, 0:P]).then_inc(done, 1)
                if item in ("q", "k"):
                    dve.wait_ge(S[item + "_hi_done"], ob + 1)
                    bias = bq_sb if item == "q" else bk_sb
                    if not first:
                        dve.wait_ge(S["qk_stored"], ob * 96)
                    dve.scalar_tensor_tensor(out=nat[item + "_lo"][:], in0=ps_m, scalar=bias[:, 0:1],
                                             in1=nat[item + "_hi"][:].bitcast(F32), op0=ALU.add,
                                             op1=ALU.subtract).then_inc(done, 1)
                if item == "ot":
                    dve.wait_ge(filled["ot"], n + 1)
                    if oc == 0 and not first:
                        dve.wait_ge(filled["on"], ob)
                    pv = ps_m.rearrange("p (n w) -> p n w", w=32)
                    dve.reciprocal(rz[:].unsqueeze(2), pv[:, :, HD:HD + 1]).then_inc(S["rz_ready"], 1)
                    dve.wait_ge(S["rz_ready"], n + 1)
                    o = o_sb[:].rearrange("p (n c d) -> p n c d", c=NG, d=HD)[:, :, oc, :]
                    dve.tensor_tensor(o, pv[:, :, 0:HD], rz[:].unsqueeze(2).to_broadcast([P, NQ * 4, HD]),
                                      ALU.mult).then_inc(done, 1)
                if item == "wo":
                    dve.wait_ge(filled["wo"], ob + 1)
                    dve.wait_ge(S["xbo_ready"], ob + 1)
                    dve.tensor_tensor(y[:].rearrange("p i d -> p (i d)"), ps_m,
                                      xbo[:].rearrange("p i d -> p (i d)"), ALU.add).then_inc(done, 1)
                    dve.wait_ge(done, ob + 1)
                    for i in range(NQ):
                        dve.bn_stats(st[:, i, :], y[:, i, :]).then_inc(S["stats_ready"], 1)
                    for i in range(NQ):
                        dve.wait_ge(S["stats_ready"], NQ * ob + i + 1)
                        dve.sem_inc(S["dve_turn"], 1)
                        dve.bn_aggr(mv[:, i, :], st[:, i, :]).then_inc(S["aggr_ready"], 1)
                if item == "lg":
                    dve.wait_ge(filled["lg"], ob + 1)
                    link = linker(S["top_link"], 15 * ob)

                    def bc(a):
                        return a.unsqueeze(2).to_broadcast([P, NQ, E])

                    dve.tensor_copy(lg[:].rearrange("p i e -> p (i e)"), ps_m[:, 0:EB]).then_inc(done, 1)
                    dve.wait_ge(done, ob + 1)
                    for k, cur in ((0, lg), (1, lg2)):
                        mx, mark = top[:, 2 * k, :], top[:, 2 * k + 1, :]
                        link(dve.tensor_reduce(mx, cur[:], AX.X, ALU.max))
                        link(dve.tensor_tensor(tmp[:], cur[:], bc(mx), ALU.is_equal))
                        link(dve.tensor_tensor(tm1[:], tmp[:], rev[:], ALU.mult))
                        link(dve.tensor_reduce(mark, tm1[:], AX.X, ALU.max))
                        link(dve.tensor_tensor(hot[k][:], rev[:], bc(mark), ALU.is_equal))
                        if k == 0:
                            link(dve.scalar_tensor_tensor(out=lg2[:], in0=hot[0][:], scalar=-3e38, in1=lg[:],
                                                          op0=ALU.mult, op1=ALU.add))
                    dve.tensor_tensor(hotb[:], hot[0][:], hot[1][:], ALU.add).then_inc(S["hot_ready"], 1)
                    link(dve.tensor_tensor(lgm[:, bass.ds(ob * EB, EB)].rearrange("p (i e) -> p i e", i=NQ), lg[:],
                                           bc(top[:, 0, :]), ALU.subtract))
                    link(dve.tensor_tensor(dm[:, bass.ds(ob * NQ, NQ)], top[:, 2, :], top[:, 0, :], ALU.subtract))
                    link(dve.tensor_copy(x1[0][:, :, D:D + 1].bitcast(I32), slot[:, 0, :].unsqueeze(2)))
                    dve.tensor_copy(x1[1][:, :, D:D + 1].bitcast(I32), slot[:, 1, :].unsqueeze(2)
                                    ).then_inc(S["x1_ids"], 1)
                    dve.wait_ge(S["x1_ids"], ob + 1)
                    link(dve.tensor_scalar(slot[:], slot[:], float(T), None, ALU.add))
                if item == "rk":
                    dve.wait_ge(filled["rk"], ob + 1)
                    link = linker(S["rank_link"], 5 * ob)
                    link(dve.tensor_tensor(rank[:], ps_m[:, 0:EB].rearrange("p (i e) -> p i e", i=NQ),
                                           nxt[:].unsqueeze(1).to_broadcast([P, NQ, E]), ALU.add))
                    dve.tensor_tensor(nxt[:], nxt[:], ps_m[:, EB:EB + E], ALU.add).then_inc(done, 1)
                    for k, t in ((0, tmp), (1, tm1)):
                        link(dve.tensor_tensor(t[:], hot[k][:], rank[:], ALU.mult))
                        link(dve.tensor_reduce(posf[:, k, :], t[:], AX.X, ALU.add))
                    if not first:
                        dve.wait_ge(S["scattered"], ob * NQ * TOPK * 16)
                    dve.tensor_copy(pos[:], posf[:]).then_inc(S["pos_ready"], 1)

            def layernorm_rows(b):
                if not (isinstance(b, int) and b == 0):
                    dve.wait_ge(S["scattered"], b * NQ * TOPK * 16)
                    dve.wait_ge(S["xr_copied"], 16 * b)
                dve.wait_ge(S["rstd_ready"], b + 1)
                for i in range(NQ):
                    dve.tensor_scalar(x1[0][:, i, 0:D], y[:, i, :], mv[:, i, 0:1], rstd[:, i:i + 1],
                                      ALU.subtract, ALU.mult).then_inc(S["x1_ready"], 1)

            def body(b):
                for c in range(NG):
                    sb_, sc_ = ahead(b, c, 2)
                    for k in range(NBANK):
                        if k in UNIT_AT and live(sb_):
                            reduce_unit(sb_, sc_, UNIT_AT[k])
                        if (c, k) in MISC:
                            shared(b, c, MISC[(c, k)])
                        if (c, k) == (2, 1) and live(b - 1):
                            layernorm_rows(b - 1)

            dve.memset(x1[0][:, :, D:ROW], 0.0)
            dve.memset(x1[1][:, :, D:ROW], 0.0)
            batches(dve, body)

            dve.wait_ge(S["iota_ready"], 7)
            dve.wait_ge(drained["rk"], B)
            tab = linker(S["tab_link"], 0)
            row = lambda n: nrow[:, n, :]
            tab(dve.tensor_copy(nrow_i[:, 0, :], nxt[0:1, :]))
            tab(dve.tensor_tensor(row(0), nxt[0:1, :], reg0[0:1, :], ALU.subtract))
            tab(dve.tensor_scalar(row(1), row(0), 1.0 / P, (P - 1.0) / P - 0.5 + 1.0 / 512, ALU.mult, ALU.add))
            tab(dve.tensor_copy(nrow_i[:, 1, :], row(1)))
            tab(dve.tensor_copy(row(2), nrow_i[:, 1, :]))
            tab(dve.memset(row(3), 1.0))
            tab(dve.tensor_tensor_scan(row(4), row(3), row(2), 0.0, ALU.mult, ALU.add))
            tab(dve.tensor_scalar(row(5), row(2), -float(P), float(REG), ALU.mult, ALU.add))
            tab(dve.tensor_tensor(tile_le[:], row(4).unsqueeze(1).to_broadcast([1, NT, E]),
                                  tile_no[:].unsqueeze(2).to_broadcast([1, NT, E]), ALU.is_le))
            tab(dve.tensor_tensor(tile_rg[:], tile_le[:], row(5).unsqueeze(1).to_broadcast([1, NT, E]), ALU.mult))
            tab(dve.tensor_reduce(tile_ef[:, 0, :], tile_le[:], AX.X, ALU.add))
            tab(dve.tensor_reduce(tile_ef[:, 1, :], tile_rg[:], AX.X, ALU.add))
            tab(dve.scalar_tensor_tensor(out=tile_ef[:, 1, :], in0=tile_no[:], scalar=float(P), in1=tile_ef[:, 1, :],
                                         op0=ALU.mult, op1=ALU.add))
            tab(dve.tensor_scalar(tile_ei[:, 0, :], tile_ef[:, 0, :], float(E - 1), None, ALU.min))
            dve.tensor_scalar(tile_ei[:, 1, :], tile_ef[:, 1, :], float(DUMP), None, ALU.min
                              ).then_inc(S["tables_ready"], 1)

            dve.wait_ge(S["gate_exp"], 2)
            gate = linker(S["gate_link"], 0)
            g = lambda n: gw[:, n, :]
            gate(dve.tensor_reduce(g(0), lgm[:].rearrange("p (t e) -> p t e", e=E), AX.X, ALU.add))
            gate(dve.reciprocal(g(1), g(0)))
            gate(dve.tensor_tensor(g(2), dm[:], g(1), ALU.mult))
            gate(dve.tensor_tensor(g(0), g(1), g(2), ALU.add))
            gate(dve.tensor_scalar(g(0), g(0), 1e-10, None, ALU.max))
            gate(dve.reciprocal(g(3), g(0)))
            gate(dve.tensor_tensor(g(4), g(1), g(3), ALU.mult))
            gate(dve.tensor_tensor(g(5), g(2), g(3), ALU.mult))

            def step(i, r):
                j, u, ii = lagged(i, r, 0)
                if tile_live(j):
                    dve.wait_ge(S["xsT_filled"], j + 1)
                    if not (isinstance(j, int) and j < 2):
                        dve.wait_ge(S["h_filled"], j - 1)
                    dve.tensor_copy(xsT[:, u % 2, :], psum[:, u % 2, 0:P]).then_inc(S["xsT_copied"], 1)
                j, u, ii = lagged(i, r, 2)
                if tile_live(j):
                    dve.wait_ge(S["hT_filled"], j + 1)
                    if not (isinstance(j, int) and j < 2):
                        dve.wait_ge(S["y_filled"], j - 1)
                    dve.tensor_copy(hT_sb[:, u % 2, :], psum[:, 4 + u % 2, 0:F]).then_inc(S["hT_copied"], 1)

            expert_steps(dve, step)

            def combine(q, u, n):
                dve.wait_ge(o_loaded[u], 32 * (n + 1))
                a = probs[:, u, 0, 0:T]
                bb = probs[:, u, 1, 0:T]
                rows = xr[:, bass.ds(q * T, T)]
                for i in range(NQ):
                    at = slice(P * i, P * i + P)
                    dve.scalar_tensor_tensor(out=a[:, at], in0=a[:, at], scalar=g(4)[:, bass.ds(q * NQ + i, 1)],
                                             in1=xr[:, bass.ds(q * T + P * i, P)], op0=ALU.mult, op1=ALU.add
                                             ).then_inc(S["comb_link"], 1)
                for i in range(NQ):
                    at = slice(P * i, P * i + P)
                    dve.wait_ge(S["comb_link"], (2 * NQ + 2) * q + i + 1)
                    dve.scalar_tensor_tensor(out=a[:, at], in0=bb[:, at], scalar=g(5)[:, bass.ds(q * NQ + i, 1)],
                                             in1=a[:, at], op0=ALU.mult, op1=ALU.add).then_inc(S["comb_link"], 1)
                dve.wait_ge(S["comb_link"], (2 * NQ + 2) * q + 2 * NQ)
                dve.tensor_scalar(a, a, 100.0, -100.0, ALU.min, ALU.max).then_inc(S["comb_link"], 1)
                dve.wait_ge(S["comb_link"], (2 * NQ + 2) * q + 2 * NQ + 1)
                dve.tensor_tensor(a, a, rows, ALU.add).then_inc(S["comb_link"], 1)
                dve.wait_ge(S["comb_link"], (2 * NQ + 2) * (q + 1))
                for i in range(NQ):
                    dve.bn_stats(st[:, i, :], a[:, P * i:P * i + P]).then_inc(S["stats_ready"], 1)
                for i in range(NQ):
                    dve.wait_ge(S["stats_ready"], NQ * B + NQ * q + i + 1)
                    dve.sem_inc(S["dve_turn"], 1)
                    dve.bn_aggr(mv[:, i, :], st[:, i, :]).then_inc(S["comb_stats"], 1)
                dve.wait_ge(S["fin_rstd"], q + 1)
                for i in range(NQ):
                    last = dve.tensor_scalar(probs[:, u, 0, 2 * T + P * i:2 * T + P * i + P], a[:, P * i:P * i + P],
                                             mv[:, i, 0:1], rstd[:, i:i + 1], ALU.subtract, ALU.mult)
                last.then_inc(S["fin_ready"], 1)

            with dve.Fori(0, B // 2) as i:
                for u in range(2):
                    combine(i * 2 + u, u, i)


_NAMES = ['x', 'xT', 'WqT', 'bq', 'WkT', 'bk', 'WvT', 'bv', 'WoT', 'bo', 'gateT', 'w1', 'b1', 'w2', 'b2']


def kernel(**inputs):
    import numpy as _np
    import concourse.bacc as _bacc
    from concourse import mybir as _mybir
    from concourse.bass_utils import run_bass_kernel_spmd as _run

    a = {k: _np.asarray(v) for k, v in inputs.items()}
    laid = {
        'x': a['L0_attn_x'], 'xT': a['L0_attn_x'].transpose(0, 2, 1),
        'WqT': a['L0_attn_Wq'].T, 'bq': a['L0_attn_bq'].reshape(-1, 1),
        'WkT': a['L0_attn_Wk'].T, 'bk': a['L0_attn_bk'].reshape(-1, 1),
        'WvT': a['L0_attn_Wv'].T, 'bv': a['L0_attn_bv'].reshape(-1, 1),
        'WoT': a['L0_attn_Wo'].T, 'bo': a['L0_attn_bo'].reshape(1, -1),
        'gateT': a['L0_ffn_gate_w'].T, 'w1': a['L0_ffn_w1'], 'b1': a['L0_ffn_b1'],
        'w2': a['L0_ffn_w2'], 'b2': a['L0_ffn_b2'],
    }
    nc = _bacc.Bacc("TRN2", target_bir_lowering=False, num_devices=1)
    arrays, args = {}, []
    for name in _NAMES:
        v = _np.ascontiguousarray(laid[name])
        arrays[f"in_{name}"] = v
        args.append(nc.dram_tensor(f"in_{name}", v.shape, _mybir.dt.from_np(v.dtype), kind="ExternalInput").ap())
    out = nc.dram_tensor("out", laid['x'].shape, F32, kind="ExternalOutput").ap()
    post_ln_attention_moe(nc, *args, out)
    r = _run(nc, [arrays], core_ids=[0])
    return r.results[0]["out"]
```

```python
from contextlib import ExitStack

import concourse.bass as bass
from concourse import mybir

ALU = mybir.AluOpType
ACT = mybir.ActivationFunctionType
AX = mybir.AxisListType
F32 = mybir.dt.float32
F32R = mybir.dt.float32r
BF16 = mybir.dt.bfloat16
I32 = mybir.dt.int32


def post_ln_attention_moe(nc, x, xT, WqT, bq, WkT, bk, WvT, bv, WoT, bo, gateT, w1, b1T, w2, b2, out):
    B, T, D = x.shape
    P = 128
    H = 16
    HD = D // H
    NQ = T // P
    NG = H // 4
    E, _, F = w1.shape
    FC = F // P
    NTOK = B * T
    TILES = NTOK // P
    TOPK = 2
    REG = NTOK + P
    ROW = D + 4
    DUMP = E * REG
    STEP = 10
    LAG = 2
    WR = 5
    FB = F + FC
    NT = -(-(NTOK * TOPK // P + E - 1) // STEP) * STEP
    SCALE = 1.0 / float(D) ** 0.5
    EPS = 1e-5
    NEG = -1e30
    NBANK = 10
    NUNIT = 6
    EB = NQ * E

    with ExitStack() as ctx:
        def sb(name, shape, dt=F32):
            return ctx.enter_context(nc.sbuf_tensor(name, shape, dt))

        def sem(name):
            return ctx.enter_context(nc.semaphore(name))

        dq = nc.dram_tensor("dq", [H, 4, HD, T], F32).ap()
        dk = nc.dram_tensor("dk", [H, 4, HD, T], F32).ap()
        xs_dram = nc.dram_tensor("xs_dram", [DUMP + P, ROW], F32).ap()
        o_dram = nc.dram_tensor("o_dram", [TOPK * NTOK, D], F32).ap()

        ident = sb("ident", [P, P])
        identb = sb("identb", [P, P], BF16)
        cmask = sb("cmask", [P, P], BF16)
        tri = sb("tri", [P, P], BF16)
        ones = sb("ones", [P, P], BF16)
        wq_sb, wk_sb, wv_sb, wo_sb = (sb(n, [P, P]) for n in ("wq_sb", "wk_sb", "wv_sb", "wo_sb"))
        gate_sb = sb("gate_sb", [P, E])
        bq_sb, bk_sb, bv_sb = (sb(n, [P, 1]) for n in ("bq_sb", "bk_sb", "bv_sb"))
        bo_bc = sb("bo_bc", [P, D])
        w1_sb = sb("w1_sb", [P, E, FB])
        w2_sb = sb("w2_sb", [P, E * F])
        b1_sb = sb("b1_sb", [P, E, FC])
        b2_bc = sb("b2_bc", [P, E * D])
        xT_sb = sb("xT_sb", [P, T])
        xTv_sb = sb("xTv_sb", [P, T])
        nat = {n: sb(n, [P, T], F32R) for n in ("q_hi", "q_lo", "k_hi", "k_lo")}
        qst = sb("qst", [P, NG, T], F32R)
        kst = sb("kst", [P, NG, 4, T], F32R)
        vst = sb("vst", [P, NQ, H, 32])
        nmax = sb("nmax", [P, NG, 16])
        nmrow = sb("nmrow", [16, 2, P], F32R)
        probs = sb("probs", [P, 2, 2, 5 * T])
        oT_sb = sb("oT_sb", [P, T])
        rz = sb("rz", [P, NQ * 4])
        o_sb = sb("o_sb", [P, T])
        onT_sb = sb("onT_sb", [P, T])
        xb = sb("xb", [P, NQ, D])
        xbo = sb("xbo", [P, NQ, D])
        y = sb("y", [P, NQ, D])
        st = sb("st", [P, NQ, 6])
        mv = sb("mv", [P, NQ, 2])
        rstd = sb("rstd", [P, NQ])
        vpe = sb("vpe", [P, NQ])
        mhalf = sb("mhalf", [P, NQ])
        x1 = [sb("x1_first", [P, NQ, ROW]), sb("x1_second", [P, NQ, ROW])]
        x1T_sb = sb("x1T_sb", [P, T])
        xr = sb("xr", [P, TILES * D])
        rev = sb("rev", [P, NQ, E])
        lg = sb("lg", [P, NQ, E])
        lg2 = sb("lg2", [P, NQ, E])
        tmp = sb("tmp", [P, NQ, E])
        tm1 = sb("tm1", [P, NQ, E])
        top = sb("top", [P, 4, NQ])
        hot = [sb("hot_first", [P, NQ, E]), sb("hot_second", [P, NQ, E])]
        hotb = sb("hotb", [P, NQ, E], BF16)
        rank = sb("rank", [P, NQ, E])
        nxt = sb("nxt", [P, E])
        reg0 = sb("reg0", [P, E])
        posf = sb("posf", [P, TOPK, NQ])
        pos = sb("pos", [P, TOPK, NQ], I32)
        slot = sb("slot", [P, TOPK, NQ])
        lgm = sb("lgm", [P, TILES * E])
        dm = sb("dm", [P, TILES])
        tabs = sb("tabs", [P, 5, E])
        tabs_i = sb("tabs_i", [P, E], I32)
        first_free = sb("first_free", [1, E], I32)
        tile_no = sb("tile_no", [P, 1])
        tile_tab = sb("tile_tab", [P, 2])
        tile_ei = sb("tile_ei", [2, P], I32)
        pad = sb("pad", [P, ROW])
        gw = sb("gw", [P, 6, TILES])
        xs = sb("xs", [P, STEP, ROW])
        xsT = sb("xsT", [P, 2, P])
        w1_cur = sb("w1_cur", [P, WR, FB])
        hT_sb = sb("hT_sb", [P, 2, F])
        y_sb = sb("y_sb", [P, STEP, D])

        psum = ctx.enter_context(nc.psum_tensor("psum", [P, 8, T], F32))
        ps_s = psum[:, 0:4, :].rearrange("p (s k) t -> p s k t", s=2)
        ps_t = psum[:, 4:6, :]
        ps_o = psum[:, 6, :]
        ps_m = psum[:, 7, :]

        S = {n: sem(n) for n in """
            pool_turn dve_turn sp_turn const_loaded weights_loaded bias_placed tab_T
            idents_ready masks_ready iota_ready const_ready kst_zeroed scratch_src scratch_set one_row
            xT_loaded xTv_loaded x_loaded xbo_ready
            q_hi_done k_hi_done qk_stored
            m_rows st_filled exp_done s_filled s_reduced masked
            pv_filled oT_copied rz_ready
            stats_ready aggr_ready vpe_ready rstd_ready x1_ready x1_ids x1b_ready xr_copied
            top_link hot_ready rank_link pos_ready scattered
            gate_exp tab_link tables_ready padded gate_link gates_ready
            xsT_filled xsT_copied w1_copied h_filled gelu_done y_filled y_copied
            comb_link comb_stats fin_vpe fin_rstd fin_ready out_stored
            """.split()}
        ITEMS = ("m", "ot", "q", "k", "v", "on", "wo", "x1t", "lg", "rk")
        filled = {n: sem(n + "_filled") for n in ITEMS}
        drained = {n: sem(n + "_drained") for n in ITEMS}
        xs_loaded = [sem(f"xs_loaded_{r}") for r in range(STEP)]
        y_scattered = [sem(f"y_scattered_{r}") for r in range(STEP)]
        o_loaded = [sem(f"o_loaded_{u}") for u in range(2)]
        qk_loaded = [sem(f"qk_loaded_{c}") for c in range(NG)]

        MISC = {(c, 1): "m" for c in range(NG)} | {(c, 8): "ot" for c in range(NG)} | {
            (0, 2): "q", (0, 4): "k", (0, 7): "v", (1, 3): "on", (1, 6): "wo", (2, 4): "x1t", (2, 6): "lg", (3, 5): "rk"}
        UNIT_AT = {0: 0, 2: 1, 3: 2, 5: 3, 7: 4, 8: 5}
        PV_AT = 5

        def live(b):
            return not isinstance(b, int) or 0 <= b < B

        def ahead(b, c, n):
            return b + (c + n) // NG, (c + n) % NG

        def owner(b, c, item):
            if item == "m":
                bb, cc = ahead(b, c, 1)
                return bb, cc, bb * NG + cc
            if item == "ot":
                bb, cc = ahead(b, c, -1)
                return bb, cc, bb * NG + cc
            bb = b + {"q": 1, "k": 1, "v": 0}.get(item, -1)
            return bb, None, bb

        ORDER = sorted(MISC)

        def before(b, c, k):
            n = ORDER.index((c, k))
            bb = b
            for _ in range(2 * len(ORDER)):
                n -= 1
                if n < 0:
                    n, bb = len(ORDER) - 1, bb - 1
                item = MISC[ORDER[n]]
                ob, _, count = owner(bb, ORDER[n][0], item)
                if live(ob):
                    return item, count + 1
            return None

        def batches(eng, body):
            body(-1)
            body(0)
            with eng.Fori(1, B - 2) as b:
                body(b)
            body(B - 2)
            body(B - 1)
            body(B)

        def expert_steps(eng, step, lookup=None, lag=0):
            engine, row, top = lookup or (None, 0, 0)

            def fetch(i):
                if lookup is None:
                    return lambda r: None
                skip = lag if isinstance(i, int) and i == 0 else 0
                count = lag if isinstance(i, int) and i > 0 else STEP + lag - skip
                _, values = nc.values_load_multi_w_load_instructions(
                    tile_ei[row:row + 1, bass.ds(i * STEP - lag + skip, count)], engines=(engine,),
                    min_val=0, max_val=top)
                return lambda r: lambda behind: values[r + lag - behind - skip]

            of = fetch(0)
            for r in range(STEP):
                step(0, r, of(r))
            with eng.Fori(1, NT // STEP) as i:
                of = fetch(i)
                for r in range(STEP):
                    step(i, r, of(r))
            if lag:
                of = fetch(NT // STEP)
                for r in range(lag):
                    step(NT // STEP, r, of(r))

        def lagged(i, r, lag):
            ii = i - 1 if r < lag else i
            rr = (r - lag) % STEP
            return ii * STEP + rr, rr, ii

        TAB_STEPS = 14

        def tile_live(j):
            return not isinstance(j, int) or 0 <= j < NT

        def seg(g, j):
            h = g % 2
            at = {0: h * T, 1: 2 * T + h * T, 3: 2 * T + h * T + 3 * P, 2: 4 * T + h * 2 * P}[j]
            return at, T - P * j

        block = ctx.enter_context(nc.Block())

        def pad_rows(eng, engine, first, end):
            eng.wait_ge(S["tab_link"], 1)
            _, rows = nc.values_load_multi_w_load_instructions(first_free[0:1, first:end], engines=(engine,),
                                                               min_val=0, max_val=DUMP)
            for row in rows:
                eng.dma_start(xs_dram[bass.ds(row, P), :], pad[:]).then_inc(S["padded"], 16)

        @block.sync
        def _(sp):
            def hold(s, n):
                sp.wait_ge(s, n)
                if not isinstance(n, int):
                    sp.sem_inc(S["sp_turn"], 1)

            for dst, src in ((wq_sb, WqT), (wk_sb, WkT), (bq_sb, bq), (bk_sb, bk)):
                sp.dma_start(dst[:], src).then_inc(S["const_loaded"], 16)
            sp.dma_start(xT_sb[:], xT[0]).then_inc(S["xT_loaded"], 16)
            sp.dma_start(xTv_sb[:], xT[0]).then_inc(S["xTv_loaded"], 16)
            for dst, src in ((wv_sb, WvT), (wo_sb, WoT), (bv_sb, bv), (gate_sb, gateT)):
                sp.dma_start(dst[:], src).then_inc(S["weights_loaded"], 16)
            sp.dma_start(bo_bc[:], bo.to_broadcast([P, D])).then_inc(S["weights_loaded"], 16)
            sp.dma_start(b1_sb[:], b1T).then_inc(S["weights_loaded"], 16)
            sp.dma_start(b2_bc[:], b2.to_broadcast([P, E * D])).then_inc(S["weights_loaded"], 16)
            sp.wait_ge(S["scratch_src"], 2)
            zeros = probs[0:H, 0].rearrange("p a t -> p (a t)")
            for dst, src in ((dq[:, 3], zeros[:, 0:HD * T]), (dk[:, 3, 1:HD], zeros[:, 0:(HD - 1) * T]),
                             (dk[:, 3, 0:1], probs[0:H, 1, 0, 0:T])):
                sp.dma_start(dst.rearrange("h d t -> h (d t)"), src).then_inc(S["scratch_set"], 16)
            sp.dma_start(w1_sb[:, :, 0:F], w1.rearrange("e d f -> d e f")).then_inc(S["weights_loaded"], 16)
            for ch in range(FC):
                sp.dma_start(w2_sb[:].rearrange("p (e c d) -> p e c d", e=E, c=FC)[:, :, ch, :],
                             w2.rearrange("e (c p) d -> c p e d", c=FC)[ch]).then_inc(S["weights_loaded"], 16)

            def load_stacks(b, c):
                if not (isinstance(b, int) and b == 0):
                    hold(S["st_filled"], (b - 1) * NBANK * NG + (c + 1) * NBANK)
                hold(S["qk_stored"], (b + 1) * 96)
                sp.dma_start(qst[:, c, :].bitcast(F32), dq.rearrange("(g c) r d t -> c g (r d) t", c=NG)[c]).then_inc(qk_loaded[c], 16)
                for g in range(4):
                    sp.dma_start(kst[32 * g:32 * g + 32, c, g, :].bitcast(F32),
                                 dk[NG * g + c].rearrange("r d t -> (r d) t")).then_inc(qk_loaded[c], 16)

            def body(b):
                for c in range(NG):
                    nb, ncg = ahead(b, c, 3)
                    if live(nb):
                        if isinstance(nb, int) and nb == 0 and ncg == 0:
                            sp.wait_ge(S["scratch_set"], 16 * 3)
                            sp.wait_ge(S["kst_zeroed"], 2)
                        load_stacks(nb, ncg)
                    for k in range(NBANK):
                        item = MISC.get((c, k))
                        if item == "m":
                            ob, oc, n = owner(b, c, "m")
                            if live(ob):
                                hold(drained["m"], n + 1)
                                sp.dma_start(qst[24:P:32, oc, :].bitcast(F32).rearrange("g (i q) -> g i q", i=NQ),
                                             nmrow[:, oc % 2, :].bitcast(F32)
                                             ).then_inc(S["m_rows"], 16)
                    if c == 0 and live(b + 1):
                        if not (isinstance(b, int) and b < 0):
                            for cc in range(NG):
                                hold(qk_loaded[cc], (b + 1) * 80)
                        for name, d, hi_done in (("q", dq, "q_hi_done"), ("k", dk, "k_hi_done")):
                            hold(S[hi_done], b + 2)
                            hi_parts, lo_part = ((0, 1), 2) if name == "q" else ((0, 2), 1)
                            for r in hi_parts:
                                sp.dma_start(d[:, r],
                                             nat[name + "_hi"][:].bitcast(F32)).then_inc(S["qk_stored"], 16)
                            hold(drained[name], b + 2)
                            sp.dma_start(d[:, lo_part],
                                         nat[name + "_lo"][:].bitcast(F32)).then_inc(S["qk_stored"], 16)
                        if live(b + 2):
                            hold(filled["k"], b + 2)
                            sp.dma_start(xT_sb[:], xT[bass.ds(b + 2, 1)].rearrange("b d t -> (b d) t")).then_inc(S["xT_loaded"], 16)
                    if c == 1 and live(b) and live(b + 1):
                        hold(filled["v"], b + 1)
                        sp.dma_start(xTv_sb[:], xT[bass.ds(b + 1, 1)].rearrange("b d t -> (b d) t")).then_inc(S["xTv_loaded"], 16)
                    if c == 2 and live(b):
                        if not (isinstance(b, int) and b == 0):
                            hold(S["xbo_ready"], b)
                        sp.dma_start(xb[:], x[bass.ds(b, 1)].rearrange("b (i p) d -> p (b i) d", p=P)).then_inc(S["x_loaded"], 16)
                    if c == 2 and live(b - 1):
                        hold(S["x1_ready"], b * NQ)
                        sp.dma_start(xr[:, bass.ds((b - 1) * T, T)].rearrange("p (i d) -> p i d", i=NQ),
                                     x1[0][:, :, 0:D]).then_inc(S["xr_copied"], 16)

            batches(sp, body)

            pad_rows(sp, mybir.EngineType.SP, 0, E // 2)
            sp.dma_start(xs_dram[DUMP:DUMP + P, :], pad[:]).then_inc(S["padded"], 16)
            sp.wait_ge(S["padded"], 16 * (E + 1))
            sp.wait_ge(S["scattered"], B * NQ * TOPK * 16)
            sp.wait_ge(S["tables_ready"], 1)

            def step(i, r, of):
                if not (isinstance(i, int) and i == 0):
                    hold(y_scattered[r], 16 * i)
                sp.dma_start(xs[:, r, :], xs_dram[bass.ds(of(0), P), :]).then_inc(xs_loaded[r], 16)

            expert_steps(sp, step, (mybir.EngineType.SP, 1, DUMP))

            for n in range(STEP):
                sp.wait_ge(y_scattered[n], 16 * NT // STEP)

            def load_results(q, u):
                for k in range(TOPK):
                    sp.dma_start(probs[:, u, k, 0:T].rearrange("p (i d) -> p i d", i=NQ),
                                 o_dram[bass.ds(q * T + k * NTOK, T), :].rearrange("(i p) d -> p i d", p=P)
                                 ).then_inc(o_loaded[u], 16)

            def store(q, u):
                hold(S["fin_ready"], q + 1)
                sp.dma_start(out[bass.ds(q, 1)].rearrange("b (i p) d -> p (b i) d", p=P),
                             probs[:, u, 0, 2 * T:3 * T].rearrange("p (i d) -> p i d", i=NQ)).then_inc(S["out_stored"], 16)

            load_results(0, 0)
            load_results(1, 1)
            with sp.Fori(0, B // 2 - 1) as i:
                for u in range(2):
                    store(i * 2 + u, u)
                    load_results(i * 2 + u + 2, u)
            store(B - 2, 0)
            store(B - 1, 1)
            sp.wait_ge(S["out_stored"], 16 * B)

        @block.gpsimd
        def _(pool):
            pool.memset(kst[:, 0:2].bitcast(F32), 0.0).then_inc(S["kst_zeroed"], 1)
            pool.memset(ident[:], 0.0).then_inc(S["idents_ready"], 1)
            pool.memset(identb[:], 0.0).then_inc(S["idents_ready"], 1)
            pool.memset(cmask[:], 0.0).then_inc(S["masks_ready"], 1)
            pool.memset(tri[:], 1.0).then_inc(S["masks_ready"], 1)
            pool.wait_ge(S["idents_ready"], 2)
            for m in (ident, identb):
                pool.affine_select(out=m[:], in_=m[:], compare_op=ALU.not_equal, fill=1.0, base=0,
                                   pattern=[[-1, P]], channel_multiplier=1).then_inc(S["idents_ready"], 1)
            pool.wait_ge(S["masks_ready"], 2)
            pool.affine_select(out=cmask[:], in_=cmask[:], compare_op=ALU.is_ge, fill=NEG, base=0,
                               pattern=[[-1, P]], channel_multiplier=1).then_inc(S["masks_ready"], 1)
            pool.affine_select(out=tri[:], in_=tri[:], compare_op=ALU.is_gt, fill=0.0, base=0,
                               pattern=[[1, P]], channel_multiplier=-1).then_inc(S["masks_ready"], 1)
            pool.iota(rev[:], [[0, NQ], [-1, E]], base=E, channel_multiplier=0,
                      allow_small_or_imprecise_dtypes=True).then_inc(S["iota_ready"], 1)
            pool.iota(nxt[:], [[REG, E]], base=0, channel_multiplier=0,
                      allow_small_or_imprecise_dtypes=True).then_inc(S["iota_ready"], 1)
            pool.iota(slot[:], [[NTOK, TOPK], [P, NQ]], base=0, channel_multiplier=1,
                      allow_small_or_imprecise_dtypes=True).then_inc(S["iota_ready"], 1)
            pool.iota(tile_no[:], [[0, 1]], base=0, channel_multiplier=1,
                      allow_small_or_imprecise_dtypes=True).then_inc(S["iota_ready"], 1)
            pool.memset(pad[:, 0:D], 0.0).then_inc(S["iota_ready"], 1)
            pool.iota(pad[:, D:ROW].bitcast(I32), [[0, ROW - D]], base=TOPK * NTOK,
                      channel_multiplier=1).then_inc(S["iota_ready"], 1)
            pool.iota(reg0[:], [[REG, E]], base=0, channel_multiplier=0,
                      allow_small_or_imprecise_dtypes=True).then_inc(S["iota_ready"], 1)
            pool.memset(mhalf[:], -0.5).then_inc(S["const_ready"], 1)

            def turn():
                pool.sem_inc(S["pool_turn"], 1)

            def body(b):
                for c in range(NG):
                    if live(b):
                        n = (b * NG + c) * NBANK
                        for p in range(2):
                            pr = probs[:, c % 2, p, :]
                            for upto, view in (
                                    (4, pr[:, 0:4 * T].rearrange("p (n t) -> p n t", t=T)[:, :, 0:P]),
                                    (4, pr[:, 2 * T:4 * T].rearrange("p (n t) -> p n t", t=T)[:, :, 3 * P:4 * P]),
                                    (5, pr[:, 4 * T:5 * T].rearrange("p (n t) -> p n t", t=2 * P)[:, :, 0:P])):
                                pool.wait_ge(S["exp_done"], n + 5 * p + upto)
                                turn()
                                pool.affine_select(out=view, in_=view, compare_op=ALU.is_ge, fill=0.0, base=0,
                                                   pattern=[[0, view.shape[1]], [1, P]], channel_multiplier=-1
                                                   ).then_inc(S["masked"], 1)
                    if c == 2 and live(b):
                        pool.wait_ge(S["x_loaded"], 16 * (b + 1))
                        turn()
                        if not (isinstance(b, int) and b == 0):
                            pool.wait_ge(drained["wo"], b)
                            turn()
                        else:
                            pool.wait_ge(S["weights_loaded"], 16 * 10)
                        pool.tensor_tensor(xbo[:], xb[:], bo_bc[:].unsqueeze(1).to_broadcast([P, NQ, D]),
                                           ALU.add).then_inc(S["xbo_ready"], 1)
                    if c == 1 and live(b - 1):
                        pool.wait_ge(S["aggr_ready"], NQ * b)
                        turn()
                        pool.tensor_scalar(vpe[:], mv[:, :, 1], EPS, None, ALU.add).then_inc(S["vpe_ready"], 1)
                        pool.wait_ge(S["vpe_ready"], b)
                        turn()
                        pool.tensor_tensor(rstd[:], vpe[:], mhalf[:], ALU.pow).then_inc(S["rstd_ready"], 1)
                    if c == 3 and live(b - 1):
                        pool.wait_ge(S["pos_ready"], b)
                        turn()
                        pool.wait_ge(S["x1_ids"], b)
                        turn()
                        pool.wait_ge(S["x1b_ready"], b)
                        turn()
                        for k in range(TOPK):
                            for i in range(NQ):
                                turn()
                                pool.indirect_dma_start(
                                    xs_dram, bass.IndirectOffsetOnAxis(pos[:, k, i:i + 1], 0), x1[k][:, i, :], None,
                                    bounds_check=DUMP - 1).then_inc(S["scattered"], 16)

            batches(pool, body)

            def step(i, r, of):
                j, u, _ = lagged(i, r, LAG)
                if not tile_live(j):
                    return
                pool.wait_ge(S["y_copied"], j + 1)
                turn()
                pool.indirect_dma_start(
                    o_dram, bass.IndirectOffsetOnAxis(xs[:, u, D:D + 1].bitcast(I32), 0), y_sb[:, u, :], None,
                    bounds_check=TOPK * NTOK - 1, oob_is_err=False).then_inc(y_scattered[u], 16)

            expert_steps(pool, step, None, LAG)
            with pool.Fori(0, B) as q:
                pool.wait_ge(S["comb_stats"], NQ * (q + 1))
                turn()
                pool.tensor_scalar(vpe[:], mv[:, :, 1], EPS, None, ALU.add).then_inc(S["fin_vpe"], 1)
                pool.wait_ge(S["fin_vpe"], q + 1)
                turn()
                pool.tensor_tensor(rstd[:], vpe[:], mhalf[:], ALU.pow).then_inc(S["fin_rstd"], 1)

        @block.scalar
        def _(act):
            def exp_bank(b, c, k):
                n = (b * NG + c) * NBANK + k
                act.wait_ge(S["st_filled"], n + 1)
                if k == 0 and not (isinstance(b, int) and b * NG + c < 2):
                    act.wait_ge(S["pv_filled"], b * NG + c - 1)
                p, kk = k // 5, k % 5
                act.activation(probs[:, c % 2, p, kk * T:(kk + 1) * T], ps_t[:, k % 2, :], ACT.Exp,
                               scale=SCALE).then_inc(S["exp_done"], 1)

            def split_hi(b, name, bias):
                act.wait_ge(filled[name], b + 1)
                if isinstance(b, int) and b == 0:
                    act.wait_ge(S["const_loaded"], 64)
                else:
                    act.wait_ge(S["qk_stored"], b * 96)
                act.activation(nat[name + "_hi"][:], ps_m, ACT.Identity, bias=bias[:, 0:1]
                               ).then_inc(S[name + "_hi_done"], 1)

            def body(b):
                for c in range(NG):
                    for k in range(NBANK):
                        if live(b):
                            exp_bank(b, c, k)
                        item = MISC.get((c, k))
                        if k == PV_AT:
                            ob, oc = ahead(b, c, -1)
                            if live(ob):
                                n = ob * NG + oc
                                act.wait_ge(S["pv_filled"], n + 1)
                                if not (isinstance(n, int) and n == 0):
                                    act.wait_ge(filled["ot"], n)
                                act.activation(oT_sb[:], ps_o, ACT.Copy).then_inc(S["oT_copied"], 1)
                        if item is None or not live(owner(b, c, item)[0]):
                            continue
                        ob = owner(b, c, item)[0]
                        if item == "q":
                            split_hi(ob, "q", bq_sb)
                        if item == "k":
                            split_hi(ob, "k", bk_sb)
                        if item == "v":
                            act.wait_ge(filled["v"], ob + 1)
                            if isinstance(ob, int) and ob == 0:
                                act.wait_ge(S["const_ready"], 4)
                            act.activation(vst[:].rearrange("p i h w -> p (i h) w")[:, :, 0:HD],
                                           ps_m.rearrange("p (n d) -> p n d", d=HD), ACT.Copy).then_inc(drained["v"], 1)
                        if item == "on":
                            act.wait_ge(filled["on"], ob + 1)
                            if isinstance(ob, int) and ob == 0:
                                act.wait_ge(S["weights_loaded"], 16 * 10)
                            act.activation(onT_sb[:], ps_m, ACT.Identity, bias=bv_sb[:, 0:1]).then_inc(drained["on"], 1)
                        if item == "x1t":
                            act.wait_ge(S["x1_ready"], NQ * (ob + 1))
                            act.activation(x1[1][:, :, 0:D], x1[0][:, :, 0:D], ACT.Copy).then_inc(S["x1b_ready"], 1)
                            act.wait_ge(filled["x1t"], ob + 1)
                            act.activation(x1T_sb[:], ps_m, ACT.Copy).then_inc(drained["x1t"], 1)

            batches(act, body)
            pad_rows(act, mybir.EngineType.Activation, E // 2, E)
            act.wait_ge(S["top_link"], 15 * B)
            act.activation(lgm[:], lgm[:], ACT.Exp).then_inc(S["gate_exp"], 1)
            act.activation(dm[:], dm[:], ACT.Exp).then_inc(S["gate_exp"], 1)

            def step(i, r, of):
                j, u, _ = lagged(i, r, 0)
                if tile_live(j):
                    act.wait_ge(S["xsT_filled"], j + 1)
                    if not (isinstance(j, int) and j < 2):
                        act.wait_ge(S["h_filled"], j - 1)
                    act.activation(xsT[:, u % 2, :], psum[:, u % 2, 0:P], ACT.Copy).then_inc(S["xsT_copied"], 1)
                j, u, _ = lagged(i, r, 1)
                if tile_live(j):
                    act.wait_ge(S["h_filled"], j + 1)
                    if not (isinstance(j, int) and j < 2):
                        act.wait_ge(S["y_filled"], j - 1)
                    for ch in range(FC):
                        last = act.activation(hT_sb[:, u % 2, P * ch:P * ch + P], psum[:, 2 + u % 2, P * ch:P * ch + P],
                                              ACT.Gelu, bias=w1_cur[:, u % WR, F + ch:F + ch + 1])
                    last.then_inc(S["gelu_done"], 1)

            expert_steps(act, step, None, LAG)

        @block.tensor
        def _(pe):
            pe.wait_ge(S["idents_ready"], 4)
            pe.wait_ge(S["masks_ready"], 4)
            pe.wait_ge(S["const_ready"], 4)

            def score_unit(b, c, u):
                n = (b * NG + c) * NUNIT + u
                if u == 0:
                    pe.wait_ge(qk_loaded[c], 80 * (b + 1))
                if not (isinstance(n, int) and n < 2):
                    pe.wait_ge(S["s_reduced"], n - 1)
                pair, kind = u // 3, u % 3
                for h in range(2):
                    g = 2 * pair + h
                    parts = {0: [(3, h, 0)], 1: [(2, h, 0), (0, h, 3 * P)], 2: [(1, 0, 2 * P * h)]}[kind]
                    for i, bank, at in parts:
                        w = P * (i + 1)
                        o = ps_s[:, u % 2, bank, :]
                        pe.matmul(o[:, at:at + w], qst[:, c, P * i:P * i + P], kst[:, c, g, 0:w], start=True, stop=False)
                        last = pe.matmul(o[:, at + w - P:at + w], identb[:], cmask[:], start=False, stop=True)
                last.then_inc(S["s_filled"], 1)

            def score_bank(b, c, k):
                n = (b * NG + c) * NBANK + k
                if k == 0:
                    pe.wait_ge(S["m_rows"], 16 * (b * NG + c + 1))
                if not (isinstance(n, int) and n < 2):
                    pe.wait_ge(S["exp_done"], n - 1)
                pair, kk = k // 5, k % 5
                for g in (2 * pair, 2 * pair + 1):
                    for j in range(NQ):
                        at, w = seg(g, j)
                        if at // T == kk:
                            last = pe.matmul(ps_t[:, k % 2, at % T:at % T + w], kst[:, c, g, P * j:P * j + P],
                                             qst[:, c, P * j:T], start=True, stop=True)
                last.then_inc(S["st_filled"], 1)

            def pv(b, c):
                n = b * NG + c
                pe.wait_ge(S["masked"], 6 * (n + 1))
                pe.wait_ge(drained["v"], b + 1)
                if not (isinstance(n, int) and n == 0):
                    pe.wait_ge(S["oT_copied"], n)
                for j in range(NQ):
                    for g in range(4):
                        at, w = seg(g, j)
                        last = pe.matmul(ps_o[32 * g:32 * g + 32, P * j:T], vst[:, j, 4 * g + c, :],
                                         probs[:, c % 2, g // 2, at:at + w], start=(j == 0), stop=(j == NQ - 1))
                last.then_inc(S["pv_filled"], 1)

            def shared(b, c, k, item):
                ob, oc, n = owner(b, c, item)
                if not live(ob):
                    return
                prev = before(b, c, k)
                if prev is not None:
                    pe.wait_ge(drained[prev[0]], prev[1])
                if item == "m":
                    pe.wait_ge(S["s_reduced"], NUNIT * (n + 1))
                    last = pe.transpose(ps_m[0:16, 0:P], nmax[:, oc, :], ident[:])
                if item == "ot":
                    pe.wait_ge(S["oT_copied"], n + 1)
                    for i in range(NQ):
                        last = pe.transpose(ps_m[:, P * i:P * i + P], oT_sb[:, P * i:P * i + P], ident[:])
                if item in ("q", "k"):
                    if isinstance(ob, int) and ob == 0:
                        pe.wait_ge(S["const_loaded"], 64)
                    pe.wait_ge(S["xT_loaded"], 16 * (ob + 1))
                    last = pe.matmul(ps_m, (wq_sb if item == "q" else wk_sb)[:], xT_sb[:], start=True, stop=True)
                if item == "v":
                    if isinstance(ob, int) and ob == 0:
                        pe.wait_ge(S["weights_loaded"], 16 * 10)
                    pe.wait_ge(S["xTv_loaded"], 16 * (ob + 1))
                    for i in range(NQ):
                        last = pe.matmul(ps_m[:, P * i:P * i + P], xTv_sb[:, P * i:P * i + P], wv_sb[:],
                                         start=True, stop=True)
                if item == "on":
                    pe.wait_ge(drained["ot"], NG * (ob + 1))
                    for i in range(NQ):
                        last = pe.transpose(ps_m[:, P * i:P * i + P], o_sb[:, P * i:P * i + P], ident[:])
                if item == "wo":
                    pe.wait_ge(drained["on"], ob + 1)
                    for i in range(NQ):
                        last = pe.matmul(ps_m[:, P * i:P * i + P], onT_sb[:, P * i:P * i + P], wo_sb[:],
                                         start=True, stop=True)
                if item == "x1t":
                    pe.wait_ge(S["x1_ready"], NQ * (ob + 1))
                    for i in range(NQ):
                        last = pe.transpose(ps_m[:, P * i:P * i + P], x1[0][:, i, 0:D], ident[:])
                if item == "lg":
                    pe.wait_ge(drained["x1t"], ob + 1)
                    for i in range(NQ):
                        last = pe.matmul(ps_m[:, E * i:E * i + E], x1T_sb[:, P * i:P * i + P], gate_sb[:],
                                         start=True, stop=True)
                if item == "rk":
                    pe.wait_ge(S["hot_ready"], ob + 1)
                    pe.matmul(ps_m[:, 0:EB], tri[:], hotb[:].rearrange("p i e -> p (i e)"), start=True, stop=False,
                              skip_group_check=True)
                    for i in range(NQ):
                        for o in range(i + 1, NQ):
                            pe.matmul(ps_m[:, E * o:E * o + E], ones[:], hotb[:, i, :], start=False, stop=False,
                                      skip_group_check=True)
                        last = pe.matmul(ps_m[:, EB:EB + E], ones[:], hotb[:, i, :], start=False, stop=(i == NQ - 1),
                                         skip_group_check=True)
                last.then_inc(filled[item], 1)

            def body(b):
                for c in range(NG):
                    sb_, sc_ = ahead(b, c, 2)
                    pb_, pc_ = ahead(b, c, -1)
                    for k in range(NBANK):
                        if live(b):
                            score_bank(b, c, k)
                        if k in UNIT_AT and live(sb_):
                            score_unit(sb_, sc_, UNIT_AT[k])
                        if k == PV_AT and live(pb_):
                            pv(pb_, pc_)
                        if (c, k) in MISC:
                            shared(b, c, k, MISC[(c, k)])

            batches(pe, body)
            pe.wait_ge(drained["rk"], B)
            pe.wait_ge(S["tab_link"], TAB_STEPS)
            pe.transpose(ps_m[0:2, 0:P], tile_tab[:], ident[:]).then_inc(S["tab_T"], 1)
            pe.wait_ge(S["weights_loaded"], 16 * 10)
            pe.wait_ge(S["tables_ready"], 1)

            def step(i, r, of):
                j, u, ii = lagged(i, r, 0)
                if tile_live(j):
                    pe.wait_ge(xs_loaded[r], 16 * (ii + 1))
                    if not (isinstance(j, int) and j < 2):
                        pe.wait_ge(S["xsT_copied"], j - 1)
                    pe.transpose(psum[:, r % 2, 0:P], xs[:, r, 0:D], ident[:]).then_inc(S["xsT_filled"], 1)
                j, u, ii = lagged(i, r, 1)
                if tile_live(j):
                    pe.wait_ge(S["xsT_copied"], j + 1)
                    pe.wait_ge(S["w1_copied"], j + 1)
                    if not (isinstance(j, int) and j < 2):
                        pe.wait_ge(S["gelu_done"], j - 1)
                    for ch in range(FC):
                        last = pe.matmul(psum[:, 2 + u % 2, P * ch:P * ch + P], w1_cur[:, u % WR, P * ch:P * ch + P],
                                         xsT[:, u % 2, :], start=True, stop=True)
                    last.then_inc(S["h_filled"], 1)
                j, u, ii = lagged(i, r, 2)
                if tile_live(j):
                    pe.wait_ge(S["gelu_done"], j + 1)
                    if not (isinstance(j, int) and j < 2):
                        pe.wait_ge(S["y_copied"], j - 1)
                    for ch in range(FC):
                        last = pe.matmul(psum[:, 4 + u % 2, 0:D], hT_sb[:, u % 2, P * ch:P * ch + P],
                                         w2_sb[:, bass.ds(of(2) * F + P * ch, D)], start=(ch == 0), stop=(ch == FC - 1))
                    last.then_inc(S["y_filled"], 1)

            expert_steps(pe, step, (mybir.EngineType.PE, 0, E - 1), LAG)

        @block.vector
        def _(dve):
            def linker(s, base):
                n = [0]

                def link(ins):
                    n[0] += 1
                    ins.then_inc(s, 1)
                    dve.wait_ge(s, base + n[0])
                return link

            dve.memset(probs[0:H, 0], 0.0).then_inc(S["scratch_src"], 1)
            dve.memset(probs[0:H, 1, 0, 0:T], 1.0).then_inc(S["scratch_src"], 1)
            dve.memset(kst[:, 2:4].bitcast(F32), 0.0).then_inc(S["kst_zeroed"], 1)
            dve.memset(ones[:], 1.0).then_inc(S["const_ready"], 1)
            dve.memset(vst[:, :, :, HD + 1:32], 0.0).then_inc(S["const_ready"], 1)
            dve.memset(vst[:, :, :, HD:HD + 1], 1.0).then_inc(S["const_ready"], 1)
            dve.wait_ge(S["iota_ready"], 3)

            def reduce_unit(b, c, u):
                n = (b * NG + c) * NUNIT + u
                dve.wait_ge(S["s_filled"], n + 1)
                pair, kind = u // 3, u % 3
                ps = ps_s[:, u % 2]
                mx = nmax[:, c, :].rearrange("p (g i) -> p g i", g=4)[:, 2 * pair:2 * pair + 2, :]
                if kind == 0:
                    todo = [(mx[:, :, 3], ps[:, :, :])]
                elif kind == 1:
                    todo = [(mx[:, :, 2], ps[:, :, 0:3 * P]), (mx[:, :, 0], ps[:, :, 3 * P:T])]
                else:
                    todo = [(mx[:, :, 1], ps[:, 0, :].rearrange("p (h w) -> p h w", h=2))]
                for o, i in todo:
                    last = dve.tensor_reduce(o, i, AX.X, ALU.max, negate=True)
                last.then_inc(S["s_reduced"], 1)

            def shared(b, c, item):
                ob, oc, n = owner(b, c, item)
                if not live(ob):
                    return
                first = isinstance(ob, int) and ob == 0
                done = drained[item]
                if item == "m":
                    dve.wait_ge(filled["m"], n + 1)
                    if not (isinstance(n, int) and n < 2):
                        dve.wait_ge(S["m_rows"], 16 * (n - 1))
                    dve.tensor_copy(nmrow[:, oc % 2, :], ps_m[0:16, 0:P]).then_inc(done, 1)
                if item in ("q", "k"):
                    dve.wait_ge(S[item + "_hi_done"], ob + 1)
                    bias = bq_sb if item == "q" else bk_sb
                    if not first:
                        dve.wait_ge(S["qk_stored"], ob * 96)
                    dve.scalar_tensor_tensor(out=nat[item + "_lo"][:], in0=ps_m, scalar=bias[:, 0:1],
                                             in1=nat[item + "_hi"][:].bitcast(F32), op0=ALU.add,
                                             op1=ALU.subtract).then_inc(done, 1)
                if item == "ot":
                    dve.wait_ge(filled["ot"], n + 1)
                    if oc == 0 and not first:
                        dve.wait_ge(filled["on"], ob)
                    pv = ps_m.rearrange("p (n w) -> p n w", w=32)
                    dve.reciprocal(rz[:].unsqueeze(2), pv[:, :, HD:HD + 1]).then_inc(S["rz_ready"], 1)
                    dve.wait_ge(S["rz_ready"], n + 1)
                    o = o_sb[:].rearrange("p (n c d) -> p n c d", c=NG, d=HD)[:, :, oc, :]
                    dve.tensor_tensor(o, pv[:, :, 0:HD], rz[:].unsqueeze(2).to_broadcast([P, NQ * 4, HD]),
                                      ALU.mult).then_inc(done, 1)
                if item == "wo":
                    dve.wait_ge(filled["wo"], ob + 1)
                    dve.wait_ge(S["xbo_ready"], ob + 1)
                    dve.tensor_tensor(y[:].rearrange("p i d -> p (i d)"), ps_m,
                                      xbo[:].rearrange("p i d -> p (i d)"), ALU.add).then_inc(done, 1)
                    dve.wait_ge(done, ob + 1)
                    for i in range(NQ):
                        dve.bn_stats(st[:, i, :], y[:, i, :]).then_inc(S["stats_ready"], 1)
                    for i in range(NQ):
                        dve.wait_ge(S["stats_ready"], NQ * ob + i + 1)
                        dve.sem_inc(S["dve_turn"], 1)
                        dve.bn_aggr(mv[:, i, :], st[:, i, :]).then_inc(S["aggr_ready"], 1)
                if item == "lg":
                    dve.wait_ge(filled["lg"], ob + 1)
                    link = linker(S["top_link"], 15 * ob)

                    def bc(a):
                        return a.unsqueeze(2).to_broadcast([P, NQ, E])

                    dve.tensor_copy(lg[:].rearrange("p i e -> p (i e)"), ps_m[:, 0:EB]).then_inc(done, 1)
                    dve.wait_ge(done, ob + 1)
                    for k, cur in ((0, lg), (1, lg2)):
                        mx, mark = top[:, 2 * k, :], top[:, 2 * k + 1, :]
                        link(dve.tensor_reduce(mx, cur[:], AX.X, ALU.max))
                        link(dve.tensor_tensor(tmp[:], cur[:], bc(mx), ALU.is_equal))
                        link(dve.tensor_tensor(tm1[:], tmp[:], rev[:], ALU.mult))
                        link(dve.tensor_reduce(mark, tm1[:], AX.X, ALU.max))
                        link(dve.tensor_tensor(hot[k][:], rev[:], bc(mark), ALU.is_equal))
                        if k == 0:
                            link(dve.scalar_tensor_tensor(out=lg2[:], in0=hot[0][:], scalar=-3e38, in1=lg[:],
                                                          op0=ALU.mult, op1=ALU.add))
                    dve.tensor_tensor(hotb[:], hot[0][:], hot[1][:], ALU.add).then_inc(S["hot_ready"], 1)
                    link(dve.tensor_tensor(lgm[:, bass.ds(ob * EB, EB)].rearrange("p (i e) -> p i e", i=NQ), lg[:],
                                           bc(top[:, 0, :]), ALU.subtract))
                    link(dve.tensor_tensor(dm[:, bass.ds(ob * NQ, NQ)], top[:, 2, :], top[:, 0, :], ALU.subtract))
                    link(dve.tensor_copy(x1[0][:, :, D:D + 1].bitcast(I32), slot[:, 0, :].unsqueeze(2)))
                    dve.tensor_copy(x1[1][:, :, D:D + 1].bitcast(I32), slot[:, 1, :].unsqueeze(2)
                                    ).then_inc(S["x1_ids"], 1)
                    dve.wait_ge(S["x1_ids"], ob + 1)
                    link(dve.tensor_scalar(slot[:], slot[:], float(T), None, ALU.add))
                if item == "rk":
                    dve.wait_ge(filled["rk"], ob + 1)
                    link = linker(S["rank_link"], 5 * ob)
                    link(dve.tensor_tensor(rank[:], ps_m[:, 0:EB].rearrange("p (i e) -> p i e", i=NQ),
                                           nxt[:].unsqueeze(1).to_broadcast([P, NQ, E]), ALU.add))
                    dve.tensor_tensor(nxt[:], nxt[:], ps_m[:, EB:EB + E], ALU.add).then_inc(done, 1)
                    for k, t in ((0, tmp), (1, tm1)):
                        link(dve.tensor_tensor(t[:], hot[k][:], rank[:], ALU.mult))
                        link(dve.tensor_reduce(posf[:, k, :], t[:], AX.X, ALU.add))
                    if not first:
                        dve.wait_ge(S["scattered"], ob * NQ * TOPK * 16)
                    dve.tensor_copy(pos[:], posf[:]).then_inc(S["pos_ready"], 1)

            def layernorm_rows(b):
                if not (isinstance(b, int) and b == 0):
                    dve.wait_ge(S["scattered"], b * NQ * TOPK * 16)
                    dve.wait_ge(S["xr_copied"], 16 * b)
                dve.wait_ge(S["rstd_ready"], b + 1)
                for i in range(NQ):
                    dve.tensor_scalar(x1[0][:, i, 0:D], y[:, i, :], mv[:, i, 0:1], rstd[:, i:i + 1],
                                      ALU.subtract, ALU.mult).then_inc(S["x1_ready"], 1)

            def body(b):
                for c in range(NG):
                    if isinstance(b, int) and b == 0 and c == 1:
                        dve.wait_ge(S["weights_loaded"], 16 * 10)
                        dve.tensor_copy(w1_sb[:, :, F:FB], b1_sb[:]).then_inc(S["bias_placed"], 1)
                    sb_, sc_ = ahead(b, c, 2)
                    for k in range(NBANK):
                        if k in UNIT_AT and live(sb_):
                            reduce_unit(sb_, sc_, UNIT_AT[k])
                        if (c, k) in MISC:
                            shared(b, c, MISC[(c, k)])
                        if (c, k) == (2, 1) and live(b - 1):
                            layernorm_rows(b - 1)

            dve.memset(x1[0][:, :, D:ROW], 0.0)
            dve.memset(x1[1][:, :, D:ROW], 0.0)
            batches(dve, body)

            dve.wait_ge(S["iota_ready"], 7)
            dve.wait_ge(drained["rk"], B)
            tab = linker(S["tab_link"], 0)
            rows_of, tiles_of, upto, step_to = (tabs[:, n, :] for n in range(4))
            tab(dve.tensor_copy(first_free[:], nxt[0:1, :]))
            tab(dve.tensor_tensor(rows_of, nxt[:], reg0[:], ALU.subtract))
            tab(dve.tensor_scalar(rows_of, rows_of, 1.0 / P, (P - 1.0) / P - 0.5 + 1.0 / 512, ALU.mult, ALU.add))
            tab(dve.tensor_copy(tabs_i[:], rows_of))
            tab(dve.tensor_copy(tiles_of, tabs_i[:]))
            tab(dve.memset(rows_of, 1.0))
            tab(dve.tensor_tensor_scan(upto, rows_of, tiles_of, 0.0, ALU.mult, ALU.add))
            tab(dve.tensor_scalar(step_to, tiles_of, -float(P), float(REG), ALU.mult, ALU.add))
            passed, moved = tabs[:, 0, :], tabs[:, 1, :]
            tab(dve.tensor_scalar(passed, upto, tile_no[:, 0:1], None, ALU.is_le))
            tab(dve.tensor_tensor(moved, passed, step_to, ALU.mult))
            tab(dve.tensor_reduce(tile_tab[:], tabs[:, 0:2, :], AX.X, ALU.add))
            tab(dve.scalar_tensor_tensor(out=tile_tab[:, 1:2], in0=tile_no[:], scalar=float(P), in1=tile_tab[:, 1:2],
                                         op0=ALU.mult, op1=ALU.add))
            tab(dve.tensor_scalar(tile_tab[:, 0:1], tile_tab[:, 0:1], float(E - 1), None, ALU.min))
            tab(dve.tensor_scalar(tile_tab[:, 1:2], tile_tab[:, 1:2], float(DUMP), None, ALU.min))
            dve.wait_ge(S["tab_T"], 1)
            dve.tensor_copy(tile_ei[:], ps_m[0:2, 0:P]).then_inc(S["tables_ready"], 1)
            dve.wait_ge(S["tables_ready"], 1)
            dve.wait_ge(S["bias_placed"], 1)

            def step(i, r, of):
                j, u, ii = lagged(i, r, 0)
                if tile_live(j):
                    if not (isinstance(j, int) and j < WR):
                        dve.wait_ge(S["gelu_done"], j - WR + 1)
                    dve.tensor_copy(w1_cur[:, u % WR, :], w1_sb[:, bass.ds(of(0), 1), :].rearrange("p e f -> p (e f)")
                                    ).then_inc(S["w1_copied"], 1)
                j, u, ii = lagged(i, r, 2)
                if tile_live(j):
                    dve.wait_ge(S["y_filled"], j + 1)
                    dve.tensor_tensor(y_sb[:, u, :], psum[:, 4 + u % 2, 0:D], b2_bc[:, bass.ds(of(2) * D, D)],
                                      ALU.add).then_inc(S["y_copied"], 1)

            expert_steps(dve, step, (mybir.EngineType.DVE, 0, E - 1), LAG)

            dve.wait_ge(S["gate_exp"], 2)
            gate = linker(S["gate_link"], 0)
            g = lambda n: gw[:, n, :]
            gate(dve.tensor_reduce(g(0), lgm[:].rearrange("p (t e) -> p t e", e=E), AX.X, ALU.add))
            gate(dve.reciprocal(g(1), g(0)))
            gate(dve.tensor_tensor(g(2), dm[:], g(1), ALU.mult))
            gate(dve.tensor_tensor(g(0), g(1), g(2), ALU.add))
            gate(dve.tensor_scalar(g(0), g(0), 1e-10, None, ALU.max))
            gate(dve.reciprocal(g(3), g(0)))
            gate(dve.tensor_tensor(g(4), g(1), g(3), ALU.mult))
            gate(dve.tensor_tensor(g(5), g(2), g(3), ALU.mult))

            def combine(q, u, n):
                dve.wait_ge(o_loaded[u], 32 * (n + 1))
                a = probs[:, u, 0, 0:T]
                bb = probs[:, u, 1, 0:T]
                rows = xr[:, bass.ds(q * T, T)]
                for i in range(NQ):
                    at = slice(P * i, P * i + P)
                    dve.scalar_tensor_tensor(out=a[:, at], in0=a[:, at], scalar=g(4)[:, bass.ds(q * NQ + i, 1)],
                                             in1=xr[:, bass.ds(q * T + P * i, P)], op0=ALU.mult, op1=ALU.add
                                             ).then_inc(S["comb_link"], 1)
                for i in range(NQ):
                    at = slice(P * i, P * i + P)
                    dve.wait_ge(S["comb_link"], (2 * NQ + 2) * q + i + 1)
                    dve.scalar_tensor_tensor(out=a[:, at], in0=bb[:, at], scalar=g(5)[:, bass.ds(q * NQ + i, 1)],
                                             in1=a[:, at], op0=ALU.mult, op1=ALU.add).then_inc(S["comb_link"], 1)
                dve.wait_ge(S["comb_link"], (2 * NQ + 2) * q + 2 * NQ)
                dve.tensor_scalar(a, a, 100.0, -100.0, ALU.min, ALU.max).then_inc(S["comb_link"], 1)
                dve.wait_ge(S["comb_link"], (2 * NQ + 2) * q + 2 * NQ + 1)
                dve.tensor_tensor(a, a, rows, ALU.add).then_inc(S["comb_link"], 1)
                dve.wait_ge(S["comb_link"], (2 * NQ + 2) * (q + 1))
                for i in range(NQ):
                    dve.bn_stats(st[:, i, :], a[:, P * i:P * i + P]).then_inc(S["stats_ready"], 1)
                for i in range(NQ):
                    dve.wait_ge(S["stats_ready"], NQ * B + NQ * q + i + 1)
                    dve.sem_inc(S["dve_turn"], 1)
                    dve.bn_aggr(mv[:, i, :], st[:, i, :]).then_inc(S["comb_stats"], 1)
                dve.wait_ge(S["fin_rstd"], q + 1)
                for i in range(NQ):
                    last = dve.tensor_scalar(probs[:, u, 0, 2 * T + P * i:2 * T + P * i + P], a[:, P * i:P * i + P],
                                             mv[:, i, 0:1], rstd[:, i:i + 1], ALU.subtract, ALU.mult)
                last.then_inc(S["fin_ready"], 1)

            with dve.Fori(0, B // 2) as i:
                for u in range(2):
                    combine(i * 2 + u, u, i)


_NAMES = ['x', 'xT', 'WqT', 'bq', 'WkT', 'bk', 'WvT', 'bv', 'WoT', 'bo', 'gateT', 'w1', 'b1T', 'w2', 'b2']


def kernel(**inputs):
    import numpy as _np
    import concourse.bacc as _bacc
    from concourse import mybir as _mybir
    from concourse.bass_utils import run_bass_kernel_spmd as _run

    a = {k: _np.asarray(v) for k, v in inputs.items()}
    laid = {
        'x': a['L0_attn_x'], 'xT': a['L0_attn_x'].transpose(0, 2, 1),
        'WqT': a['L0_attn_Wq'].T, 'bq': a['L0_attn_bq'].reshape(-1, 1),
        'WkT': a['L0_attn_Wk'].T, 'bk': a['L0_attn_bk'].reshape(-1, 1),
        'WvT': a['L0_attn_Wv'].T, 'bv': a['L0_attn_bv'].reshape(-1, 1),
        'WoT': a['L0_attn_Wo'].T, 'bo': a['L0_attn_bo'].reshape(1, -1),
        'gateT': a['L0_ffn_gate_w'].T, 'w1': a['L0_ffn_w1'], 'b1T': a['L0_ffn_b1'].reshape(a['L0_ffn_b1'].shape[0], -1, 128).transpose(2, 0, 1),
        'w2': a['L0_ffn_w2'], 'b2': a['L0_ffn_b2'].reshape(1, -1),
    }
    nc = _bacc.Bacc("TRN2", target_bir_lowering=False, num_devices=1)
    arrays, args = {}, []
    for name in _NAMES:
        v = _np.ascontiguousarray(laid[name])
        arrays[f"in_{name}"] = v
        args.append(nc.dram_tensor(f"in_{name}", v.shape, _mybir.dt.from_np(v.dtype), kind="ExternalInput").ap())
    out = nc.dram_tensor("out", laid['x'].shape, F32, kind="ExternalOutput").ap()
    post_ln_attention_moe(nc, *args, out)
    r = _run(nc, [arrays], core_ids=[0])
    return r.results[0]["out"]
```

```python
from contextlib import ExitStack

import concourse.bass as bass
from concourse import mybir

ALU = mybir.AluOpType
ACT = mybir.ActivationFunctionType
AX = mybir.AxisListType
F32 = mybir.dt.float32
F32R = mybir.dt.float32r
BF16 = mybir.dt.bfloat16
I32 = mybir.dt.int32


def post_ln_attention_moe(nc, x, xT, WqT, bq, WkT, bk, WvT, bv, WoT, bo, gateT, w1, b1T, w2, b2, out):
    B, T, D = x.shape
    P = 128
    H = 16
    HD = D // H
    NQ = T // P
    NG = H // 4
    E, _, F = w1.shape
    FC = F // P
    NTOK = B * T
    TILES = NTOK // P
    TOPK = 2
    REG = NTOK + P
    ROW = D + 4
    DUMP = E * REG
    STEP = 16
    LAG = 2
    LOOK = 4
    WR = 4
    B1_AT, W2_AT, B2_AT, WCOLS = F, F + FC, 2 * F + FC, 2 * F + FC + D
    FIN = 4
    FIN_LAG = 2
    NT = NTOK * TOPK // P + E - 1
    SCALE = 1.0 / float(D) ** 0.5
    EPS = 1e-5
    NEG = -1e30
    NBANK = 10
    NUNIT = 6
    EB = NQ * E

    with ExitStack() as ctx:
        def sb(name, shape, dt=F32):
            return ctx.enter_context(nc.sbuf_tensor(name, shape, dt))

        def sem(name):
            return ctx.enter_context(nc.semaphore(name))

        dq = nc.dram_tensor("dq", [H, 4, HD, T], F32).ap()
        dk = nc.dram_tensor("dk", [H, 4, HD, T], F32).ap()
        xs_dram = nc.dram_tensor("xs_dram", [DUMP + P, ROW], F32).ap()
        o_dram = nc.dram_tensor("o_dram", [TOPK * NTOK, D], F32).ap()

        ident = sb("ident", [P, P])
        cmask = sb("cmask", [P, P])
        identr, cmaskr = sb("identr", [P, P], F32R), sb("cmaskr", [P, 2, P], F32R)
        tri = sb("tri", [P, P], BF16)
        ones = sb("ones", [P, P], BF16)
        wq_sb, wk_sb, wv_sb, wo_sb = (sb(n, [P, P]) for n in ("wq_sb", "wk_sb", "wv_sb", "wo_sb"))
        gate_sb = sb("gate_sb", [P, E])
        bq_sb, bk_sb, bv_sb = (sb(n, [P, 1]) for n in ("bq_sb", "bk_sb", "bv_sb"))
        bo_bc = sb("bo_bc", [P, D])
        experts = sb("experts", [P, E, WCOLS])
        b1_sb = sb("b1_sb", [P, E, FC])
        xT_sb = sb("xT_sb", [P, T])
        xTv_sb = sb("xTv_sb", [P, T])
        nat = {n: sb(n, [P, T], F32R) for n in ("q_hi", "q_lo", "k_hi", "k_lo")}
        qst = sb("qst", [P, NG, T], F32R)
        kst = sb("kst", [P, NG, 4, T], F32R)
        vst = sb("vst", [P, NQ, H, 32])
        nmax = sb("nmax", [P, NG, 16])
        nmrow = sb("nmrow", [16, 2, P], F32R)
        probs = sb("probs", [P, 2, 2, 5 * T])
        oT_sb = sb("oT_sb", [P, T])
        rz = sb("rz", [P, NQ * 4])
        o_sb = sb("o_sb", [P, T])
        onT_sb = sb("onT_sb", [P, T])
        xb = sb("xb", [P, NQ, D])
        xbo = sb("xbo", [P, NQ, D])
        y = sb("y", [P, NQ, D])
        st = sb("st", [P, NQ, 6])
        mv = sb("mv", [P, NQ, 2])
        rstd = sb("rstd", [P, NQ])
        vpe = sb("vpe", [P, NQ])
        mhalf = sb("mhalf", [P, NQ])
        x1 = [sb("x1_first", [P, NQ, ROW]), sb("x1_second", [P, NQ, ROW])]
        x1T_sb = sb("x1T_sb", [P, T])
        xr = sb("xr", [P, TILES * D])
        rev = sb("rev", [P, NQ, E])
        lg = sb("lg", [P, NQ, E])
        lg2 = sb("lg2", [P, NQ, E])
        tmp = sb("tmp", [P, NQ, E])
        tm1 = sb("tm1", [P, NQ, E])
        top = sb("top", [P, 4, NQ])
        hot = [sb("hot_first", [P, NQ, E]), sb("hot_second", [P, NQ, E])]
        hotb = sb("hotb", [P, NQ, E], BF16)
        rank = sb("rank", [P, NQ, E])
        nxt = sb("nxt", [P, E])
        reg0 = sb("reg0", [P, E])
        posf = sb("posf", [P, TOPK, NQ])
        pos = sb("pos", [P, TOPK, NQ], I32)
        slot = sb("slot", [P, TOPK, NQ])
        lgm = sb("lgm", [P, TILES * E])
        dm = sb("dm", [P, TILES])
        tabs = sb("tabs", [P, 4, E])
        tabs_i = sb("tabs_i", [P, E], I32)
        first_free = sb("first_free", [1, E], I32)
        tile_no = sb("tile_no", [P, 1])
        tile_tab = sb("tile_tab", [P, 2])
        tile_ei = sb("tile_ei", [2, P], I32)
        pad = sb("pad", [P, ROW])
        gw = sb("gw", [P, 6, TILES])
        xs = sb("xs", [P, STEP, ROW])
        xsT = sb("xsT", [P, 2, P])
        w_cur = sb("w_cur", [P, WR, WCOLS])
        hT_sb = sb("hT_sb", [P, 2, F])
        y_sb = probs[:, 0, 0, 0:STEP * D].rearrange("p (n d) -> p n d", d=D)

        fin = probs[:].rearrange("p u h t -> p (u h t)")[:, 0:FIN * 3 * T].rearrange("p (n k t) -> p n k t", n=FIN, k=3)
        diag = probs[:].rearrange("p u h t -> p (u h t)")[:, FIN * 3 * T:(FIN * 3 + 4) * T].rearrange(
            "p (n k i w) -> p n k i w", n=2, k=TOPK, i=NQ)
        fin_st = sb("fin_st", [P, 2, NQ, 6])
        fin_mv = sb("fin_mv", [P, 2, NQ, 2])
        fin_rs = sb("fin_rs", [P, 2, NQ])

        psum = ctx.enter_context(nc.psum_tensor("psum", [P, 8, T], F32))
        ps_s = psum[:, 0:4, :].rearrange("p (s k) t -> p s k t", s=2)
        ps_t = psum[:, 4:6, :]
        ps_o = psum[:, 6, :]
        ps_m = psum[:, 7, :]

        S = {n: sem(n) for n in """
            pool_turn dve_turn sp_turn const_loaded weights_loaded experts_loaded bias_placed tab_T
            idents_ready masks_ready iota_ready const_ready kst_zeroed scratch_src scratch_set 
            xT_loaded xTv_loaded x_loaded xbo_ready
            q_hi_done k_hi_done qk_stored
            m_rows st_filled exp_done s_filled s_reduced masked
            pv_filled oT_copied rz_ready
            stats_ready aggr_ready vpe_ready rstd_ready x1_ready x1_ids x1b_ready xr_copied
            top_link hot_ready rank_link pos_ready scattered
            gate_exp tab_link tables_ready padded gate_link 
            xsT_filled xsT_copied w_copied h_filled gelu_done y_filled y_copied
            diag_ready summed clipped residual_added fin_stats fin_aggr fin_vpe fin_rstd fin_ready
            """.split()}
        ITEMS = ("m", "ot", "q", "k", "v", "on", "wo", "x1t", "lg", "rk")
        filled = {n: sem(n + "_filled") for n in ITEMS}
        drained = {n: sem(n + "_drained") for n in ITEMS}
        xs_loaded = [sem(f"xs_loaded_{r}") for r in range(STEP)]
        y_scattered = [sem(f"y_scattered_{r}") for r in range(STEP)]
        o_loaded = [sem(f"o_loaded_{u}") for u in range(FIN)]
        out_stored = [sem(f"out_stored_{u}") for u in range(FIN)]
        qk_loaded = [sem(f"qk_loaded_{c}") for c in range(NG)]

        MISC = {
            (0, 1): "m", (0, 3): "q", (0, 5): "k", (0, 7): "v", (0, 9): "ot",
            (1, 1): "m", (1, 2): "on", (1, 4): "wo", (1, 9): "ot",
            (2, 1): "m", (2, 2): "x1t", (2, 4): "lg", (2, 9): "ot",
            (3, 1): "m", (3, 3): "rk", (3, 9): "ot"}
        LN_AT = (1, 6)
        TOP_AT = {(2, 5): (0, 1, 2, 3), (2, 6): (4, 5), (3, 1): (6,)}
        RANK_AT = {(3, 4): (0, 1, 2)}
        UNIT_AT = {0: 0, 2: 1, 3: 2, 5: 3, 7: 4, 8: 5}
        PV_AT = 5

        def live(b):
            return not isinstance(b, int) or 0 <= b < B

        def ahead(b, c, n):
            return b + (c + n) // NG, (c + n) % NG

        def owner(b, c, item):
            if item == "m":
                bb, cc = ahead(b, c, 1)
                return bb, cc, bb * NG + cc
            if item == "ot":
                bb, cc = ahead(b, c, -1)
                return bb, cc, bb * NG + cc
            bb = b + {"q": 1, "k": 1, "v": 0}.get(item, -1)
            return bb, None, bb

        ORDER = sorted(MISC)

        def before(b, c, k):
            n = ORDER.index((c, k))
            bb = b
            for _ in range(2 * len(ORDER)):
                n -= 1
                if n < 0:
                    n, bb = len(ORDER) - 1, bb - 1
                item = MISC[ORDER[n]]
                ob, _, count = owner(bb, ORDER[n][0], item)
                if live(ob):
                    return item, count + 1
            return None

        def batches(eng, body):
            body(-1)
            body(0)
            with eng.Fori(1, B - 2) as b:
                body(b)
            body(B - 2)
            body(B - 1)
            body(B)

        def pipeline(eng, step, count, unroll, lag, lookup=None):
            def body(i, steps):
                found = [None] * (steps + LOOK)
                for r in range(steps):
                    if lookup and r % LOOK == 0:
                        engine, row, top = lookup
                        _, found[r:r + LOOK] = nc.values_load_multi_w_load_instructions(
                            tile_ei[row:row + 1, bass.ds(i * STEP + r, LOOK)], engines=(engine,),
                            min_val=0, max_val=top,
                            skip_runtime_bounds_check_because="the table's entries are clamped as they are made")
                    step(i, r, found[r])

            body(0, unroll)
            with eng.Fori(1, count // unroll) as i:
                body(i, unroll)
            body(count // unroll, count % unroll)
            for r in range(count % unroll, count % unroll + lag):
                step(count // unroll, r, None)

        def expert_steps(eng, step, lag, lookup=None):
            pipeline(eng, step, NT, STEP, lag, lookup)

        def lagged(i, r, lag, unroll=STEP):
            if isinstance(i, int):
                j = i * unroll + r - lag
                return j, j % unroll, j // unroll
            ii = i - 1 if r < lag else i
            rr = (r - lag) % unroll
            return ii * unroll + rr, rr, ii

        TAB_STEPS = 14

        def tile_live(j, count=NT):
            return not isinstance(j, int) or 0 <= j < count

        def seg(g, j):
            h = g % 2
            at = {0: h * T, 1: 2 * T + h * T, 3: 2 * T + h * T + 3 * P, 2: 4 * T + h * 2 * P}[j]
            return at, T - P * j

        def pad_rows(eng, engine, first, end):
            eng.wait_ge(S["tab_link"], 1)
            _, rows = nc.values_load_multi_w_load_instructions(
                first_free[0:1, first:end], engines=(engine,), min_val=0, max_val=DUMP,
                skip_runtime_bounds_check_because="a region holds every token and a tile more")
            for row in rows:
                eng.dma_start(xs_dram[bass.ds(row, P), :], pad[:]).then_inc(S["padded"], 16)

        block = ctx.enter_context(nc.Block())

        @block.sync
        def _(sp):
            def hold(s, n):
                sp.wait_ge(s, n)
                if not isinstance(n, int):
                    sp.sem_inc(S["sp_turn"], 1)

            sp.dma_start(xT_sb[:], xT[0]).then_inc(S["xT_loaded"], 16)
            for dst, src in ((wq_sb, WqT), (wk_sb, WkT), (bq_sb, bq), (bk_sb, bk)):
                sp.dma_start(dst[:], src).then_inc(S["const_loaded"], 16)
            sp.wait_ge(S["scratch_src"], 2)
            zeros, row_of_ones = probs[0:H, 0, 0, 0:T], probs[0:H, 1, 0, 0:T]
            for dst, src, rows in ((dq[:, 3], zeros, HD), (dk[:, 3, 1:HD], zeros, HD - 1), (dk[:, 3, 0:1], row_of_ones, 1)):
                sp.dma_start(dst, src.unsqueeze(1).to_broadcast([H, rows, T])).then_inc(S["scratch_set"], 16)

            def load_weights():
                sp.dma_start(xTv_sb[:], xT[0]).then_inc(S["xTv_loaded"], 16)
                for dst, src in ((wv_sb, WvT), (wo_sb, WoT), (bv_sb, bv), (gate_sb, gateT)):
                    sp.dma_start(dst[:], src).then_inc(S["weights_loaded"], 16)
                sp.dma_start(bo_bc[:], bo.to_broadcast([P, D])).then_inc(S["weights_loaded"], 16)
                sp.dma_start(b1_sb[:], b1T).then_inc(S["weights_loaded"], 16)
                sp.dma_start(experts[:, :, B2_AT:WCOLS],
                             b2.to_broadcast([P, E * D]).rearrange("p (e d) -> p e d", e=E)
                             ).then_inc(S["weights_loaded"], 16)

            def load_experts():
                sp.dma_start(experts[:, :, 0:F], w1.rearrange("e d f -> d e f")).then_inc(S["experts_loaded"], 16)
                for ch in range(FC):
                    sp.dma_start(experts[:, :, W2_AT + P * ch:W2_AT + P * ch + D],
                                 w2.rearrange("e (c p) d -> c p e d", c=FC)[ch]).then_inc(S["experts_loaded"], 16)

            def load_stacks(b, c):
                if not (isinstance(b, int) and b == 0):
                    hold(S["st_filled"], (b - 1) * NBANK * NG + (c + 1) * NBANK)
                hold(S["qk_stored"], (b + 1) * 96)
                sp.dma_start(qst[:, c, :].bitcast(F32), dq.rearrange("(g c) r d t -> c g (r d) t", c=NG)[c]
                             ).then_inc(qk_loaded[c], 16)
                for g in range(4):
                    sp.dma_start(kst[32 * g:32 * g + 32, c, g, :].bitcast(F32),
                                 dk[NG * g + c].rearrange("r d t -> (r d) t")).then_inc(qk_loaded[c], 16)

            def body(b):
                for c in range(NG):
                    nb, ncg = ahead(b, c, 3)
                    if live(nb):
                        if isinstance(nb, int) and nb == 0:
                            if ncg == 0:
                                sp.wait_ge(S["scratch_set"], 16 * 3)
                            sp.wait_ge(S["kst_zeroed"], ncg + 1)
                        load_stacks(nb, ncg)
                    if isinstance(b, int) and (b, c) == (-1, 2):
                        load_weights()
                    if isinstance(b, int) and (b, c) == (0, 2):
                        load_experts()
                    for k in range(NBANK):
                        item = MISC.get((c, k))
                        if item == "m":
                            ob, oc, n = owner(b, c, "m")
                            if live(ob):
                                hold(drained["m"], n + 1)
                                sp.dma_start(qst[24:P:32, oc, :].bitcast(F32).rearrange("g (i q) -> g i q", i=NQ),
                                             nmrow[:, oc % 2, :].bitcast(F32)
                                             ).then_inc(S["m_rows"], 16)
                    if c == 0 and live(b + 1):
                        if not (isinstance(b, int) and b < 0):
                            for cc in range(NG):
                                hold(qk_loaded[cc], (b + 1) * 80)
                        for name, d, hi_done in (("q", dq, "q_hi_done"), ("k", dk, "k_hi_done")):
                            hold(S[hi_done], b + 2)
                            hi_parts, lo_part = ((0, 1), 2) if name == "q" else ((0, 2), 1)
                            for r in hi_parts:
                                sp.dma_start(d[:, r],
                                             nat[name + "_hi"][:].bitcast(F32)).then_inc(S["qk_stored"], 16)
                            hold(drained[name], b + 2)
                            sp.dma_start(d[:, lo_part],
                                         nat[name + "_lo"][:].bitcast(F32)).then_inc(S["qk_stored"], 16)
                        if live(b + 2):
                            hold(filled["k"], b + 2)
                            sp.dma_start(xT_sb[:], xT[bass.ds(b + 2, 1)].rearrange("b d t -> (b d) t")
                                         ).then_inc(S["xT_loaded"], 16)
                    if c == 1 and live(b) and live(b + 1):
                        hold(filled["v"], b + 1)
                        sp.dma_start(xTv_sb[:], xT[bass.ds(b + 1, 1)].rearrange("b d t -> (b d) t")
                                     ).then_inc(S["xTv_loaded"], 16)
                    if c == 2 and live(b):
                        if not (isinstance(b, int) and b == 0):
                            hold(S["xbo_ready"], b)
                        sp.dma_start(xb[:], x[bass.ds(b, 1)].rearrange("b (i p) d -> p (b i) d", p=P)
                                     ).then_inc(S["x_loaded"], 16)
                    if c == 2 and live(b - 1):
                        hold(S["x1_ready"], b * NQ)
                        sp.dma_start(xr[:, bass.ds((b - 1) * T, T)].rearrange("p (i d) -> p i d", i=NQ),
                                     x1[0][:, :, 0:D]).then_inc(S["xr_copied"], 16)

            batches(sp, body)

            pad_rows(sp, mybir.EngineType.SP, 0, E // 2)
            sp.dma_start(xs_dram[DUMP:DUMP + P, :], pad[:]).then_inc(S["padded"], 16)
            sp.wait_ge(S["padded"], 16 * (E + 1))
            sp.wait_ge(S["scattered"], B * NQ * TOPK * 16)
            sp.wait_ge(S["tables_ready"], 1)

            def step(i, r, found):
                if not (isinstance(i, int) and i == 0):
                    hold(y_scattered[r], 16 * i)
                sp.dma_start(xs[:, r, :], xs_dram[bass.ds(found, P), :]).then_inc(xs_loaded[r], 16)

            expert_steps(sp, step, 0, (mybir.EngineType.SP, 1, DUMP))

            for n in range(STEP):
                sp.wait_ge(y_scattered[n], 16 * -(-(NT - n) // STEP))

            def load_results(q, u):
                for k in range(TOPK):
                    sp.dma_start(fin[:, u, k, :].rearrange("p (i d) -> p i d", i=NQ),
                                 o_dram[bass.ds(q * T + k * NTOK, T), :].rearrange("(i p) d -> p i d", p=P)
                                 ).then_inc(o_loaded[u], 16)

            def fin_step(i, r, _):
                q, u, _ = lagged(i, r, 0, FIN)
                if tile_live(q, B - FIN):
                    hold(S["summed"], q + 1)
                    load_results(q + FIN, u)
                q, u, _ = lagged(i, r, FIN_LAG, FIN)
                if tile_live(q, B):
                    hold(S["fin_ready"], q + 1)
                    sp.dma_start(out[bass.ds(q, 1)].rearrange("b (i p) d -> p (b i) d", p=P),
                                 fin[:, u, 2, :].rearrange("p (i d) -> p i d", i=NQ)).then_inc(out_stored[u], 16)

            for u in range(FIN):
                load_results(u, u)
            pipeline(sp, fin_step, B, FIN, FIN_LAG)
            for u in range(FIN):
                sp.wait_ge(out_stored[u], 16 * (B // FIN))

        @block.gpsimd
        def _(pool):
            pool.memset(kst[:, 0].bitcast(F32), 0.0).then_inc(S["kst_zeroed"], 1)
            pool.memset(ident[:], 0.0).then_inc(S["idents_ready"], 1)
            pool.memset(cmask[:], 0.0).then_inc(S["masks_ready"], 1)
            pool.memset(tri[:], 1.0).then_inc(S["masks_ready"], 1)
            pool.wait_ge(S["idents_ready"], 1)
            pool.affine_select(out=ident[:], in_=ident[:], compare_op=ALU.not_equal, fill=1.0, base=0,
                               pattern=[[-1, P]], channel_multiplier=1).then_inc(S["idents_ready"], 1)
            pool.memset(kst[:, 1].bitcast(F32), 0.0).then_inc(S["kst_zeroed"], 1)
            pool.wait_ge(S["masks_ready"], 2)
            pool.affine_select(out=cmask[:], in_=cmask[:], compare_op=ALU.is_ge, fill=NEG, base=0,
                               pattern=[[-1, P]], channel_multiplier=1).then_inc(S["masks_ready"], 1)
            pool.affine_select(out=tri[:], in_=tri[:], compare_op=ALU.is_gt, fill=0.0, base=0,
                               pattern=[[1, P]], channel_multiplier=-1).then_inc(S["masks_ready"], 1)
            for c in range(2, NG):
                pool.memset(kst[:, c].bitcast(F32), 0.0).then_inc(S["kst_zeroed"], 1)
            pool.iota(rev[:], [[0, NQ], [-1, E]], base=E, channel_multiplier=0,
                      allow_small_or_imprecise_dtypes=True).then_inc(S["iota_ready"], 1)
            pool.iota(nxt[:], [[REG, E]], base=0, channel_multiplier=0,
                      allow_small_or_imprecise_dtypes=True).then_inc(S["iota_ready"], 1)
            pool.iota(slot[:], [[NTOK, TOPK], [P, NQ]], base=0, channel_multiplier=1,
                      allow_small_or_imprecise_dtypes=True).then_inc(S["iota_ready"], 1)
            pool.iota(tile_no[:], [[0, 1]], base=0, channel_multiplier=1,
                      allow_small_or_imprecise_dtypes=True).then_inc(S["iota_ready"], 1)
            pool.memset(pad[:, 0:D], 0.0).then_inc(S["iota_ready"], 1)
            pool.iota(pad[:, D:ROW].bitcast(I32), [[0, ROW - D]], base=TOPK * NTOK,
                      channel_multiplier=1).then_inc(S["iota_ready"], 1)
            pool.iota(reg0[:], [[REG, E]], base=0, channel_multiplier=0,
                      allow_small_or_imprecise_dtypes=True).then_inc(S["iota_ready"], 1)
            pool.memset(mhalf[:], -0.5).then_inc(S["const_ready"], 1)

            def turn():
                pool.sem_inc(S["pool_turn"], 1)

            def reciprocal_spread(b):
                pool.wait_ge(S["aggr_ready"], NQ * (b + 1))
                turn()
                pool.tensor_scalar(vpe[:], mv[:, :, 1], EPS, None, ALU.add).then_inc(S["vpe_ready"], 1)
                pool.wait_ge(S["vpe_ready"], b + 1)
                turn()
                pool.tensor_tensor(rstd[:], vpe[:], mhalf[:], ALU.pow).then_inc(S["rstd_ready"], 1)

            def body(b):
                for c in range(NG):
                    if live(b):
                        n = (b * NG + c) * NBANK
                        for p in range(2):
                            if c == 1 and p == 1 and live(b - 1):
                                reciprocal_spread(b - 1)
                            pr = probs[:, c % 2, p, :]
                            for upto, view in (
                                    (4, pr[:, 0:4 * T].rearrange("p (n t) -> p n t", t=T)[:, :, 0:P]),
                                    (4, pr[:, 2 * T:4 * T].rearrange("p (n t) -> p n t", t=T)[:, :, 3 * P:4 * P]),
                                    (5, pr[:, 4 * T:5 * T].rearrange("p (n t) -> p n t", t=2 * P)[:, :, 0:P])):
                                pool.wait_ge(S["exp_done"], n + 5 * p + upto)
                                turn()
                                pool.affine_select(out=view, in_=view, compare_op=ALU.is_ge, fill=0.0, base=0,
                                                   pattern=[[0, view.shape[1]], [1, P]], channel_multiplier=-1
                                                   ).then_inc(S["masked"], 1)
                    if c == 1 and not live(b) and live(b - 1):
                        reciprocal_spread(b - 1)
                    if c == 2 and live(b):
                        pool.wait_ge(S["x_loaded"], 16 * (b + 1))
                        turn()
                        if not (isinstance(b, int) and b == 0):
                            pool.wait_ge(drained["wo"], b)
                            turn()
                        else:
                            pool.wait_ge(S["weights_loaded"], 16 * 7)
                        pool.tensor_tensor(xbo[:], xb[:], bo_bc[:].unsqueeze(1).to_broadcast([P, NQ, D]),
                                           ALU.add).then_inc(S["xbo_ready"], 1)
                    if c == 3 and live(b - 1):
                        pool.wait_ge(S["pos_ready"], b)
                        turn()
                        pool.wait_ge(S["x1_ids"], b)
                        turn()
                        pool.wait_ge(S["x1b_ready"], b)
                        turn()
                        for k in range(TOPK):
                            for i in range(NQ):
                                turn()
                                pool.indirect_dma_start(
                                    xs_dram, bass.IndirectOffsetOnAxis(pos[:, k, i:i + 1], 0), x1[k][:, i, :], None,
                                    bounds_check=DUMP - 1).then_inc(S["scattered"], 16)

            batches(pool, body)

            def step(i, r, found):
                j, u, _ = lagged(i, r, LAG)
                if not tile_live(j):
                    return
                pool.wait_ge(S["y_copied"], j + 1)
                turn()
                pool.indirect_dma_start(
                    o_dram, bass.IndirectOffsetOnAxis(xs[:, u, D:D + 1].bitcast(I32), 0), y_sb[:, u, :], None,
                    bounds_check=TOPK * NTOK - 1, oob_is_err=False).then_inc(y_scattered[u], 16)

            expert_steps(pool, step, LAG)

            def fin_step(i, r, _):
                q, u, _ = lagged(i, r, 0, FIN)
                if tile_live(q, B):
                    pool.wait_ge(S["clipped"], q + 1)
                    turn()
                    pool.tensor_tensor(fin[:, u, 2, :], fin[:, u, 2, :], xr[:, bass.ds(q * T, T)], ALU.add
                                       ).then_inc(S["residual_added"], 1)
                q, u, _ = lagged(i, r, 1, FIN)
                if tile_live(q, B):
                    pool.wait_ge(S["fin_aggr"], NQ * (q + 1))
                    turn()
                    if not (isinstance(q, int) and q < 2):
                        pool.wait_ge(S["fin_ready"], q - 1)
                        turn()
                    rs = fin_rs[:, u % 2, :]
                    pool.tensor_scalar(rs, fin_mv[:, u % 2, :, 1], EPS, None, ALU.add).then_inc(S["fin_vpe"], 1)
                    pool.wait_ge(S["fin_vpe"], q + 1)
                    turn()
                    pool.tensor_tensor(rs, rs, mhalf[:], ALU.pow).then_inc(S["fin_rstd"], 1)

            pipeline(pool, fin_step, B, FIN, 1)

        @block.scalar
        def _(act):
            def exp_bank(b, c, k):
                n = (b * NG + c) * NBANK + k
                act.wait_ge(S["st_filled"], n + 1)
                if k == 0 and not (isinstance(b, int) and b * NG + c < 2):
                    act.wait_ge(S["pv_filled"], b * NG + c - 1)
                p, kk = k // 5, k % 5
                act.activation(probs[:, c % 2, p, kk * T:(kk + 1) * T], ps_t[:, k % 2, :], ACT.Exp,
                               scale=SCALE).then_inc(S["exp_done"], 1)

            def split_hi(b, name, bias):
                act.wait_ge(filled[name], b + 1)
                if isinstance(b, int) and b == 0:
                    act.wait_ge(S["const_loaded"], 64)
                else:
                    act.wait_ge(S["qk_stored"], b * 96)
                act.activation(nat[name + "_hi"][:], ps_m, ACT.Identity, bias=bias[:, 0:1]
                               ).then_inc(S[name + "_hi_done"], 1)

            def body(b):
                for c in range(NG):
                    for k in range(NBANK):
                        if live(b):
                            exp_bank(b, c, k)
                        item = MISC.get((c, k))
                        if k == PV_AT:
                            ob, oc = ahead(b, c, -1)
                            if live(ob):
                                n = ob * NG + oc
                                act.wait_ge(S["pv_filled"], n + 1)
                                if not (isinstance(n, int) and n == 0):
                                    act.wait_ge(filled["ot"], n)
                                act.activation(oT_sb[:], ps_o, ACT.Copy).then_inc(S["oT_copied"], 1)
                        if item is None or not live(owner(b, c, item)[0]):
                            continue
                        ob = owner(b, c, item)[0]
                        if item == "m":
                            _, oc, n = owner(b, c, "m")
                            act.wait_ge(filled["m"], n + 1)
                            if not (isinstance(n, int) and n < 2):
                                act.wait_ge(S["m_rows"], 16 * (n - 1))
                            act.activation(nmrow[:, oc % 2, :], ps_m[0:16, 0:P], ACT.Copy).then_inc(drained["m"], 1)
                        if item == "q":
                            split_hi(ob, "q", bq_sb)
                        if item == "k":
                            split_hi(ob, "k", bk_sb)
                        if item == "v":
                            act.wait_ge(filled["v"], ob + 1)
                            if isinstance(ob, int) and ob == 0:
                                act.wait_ge(S["const_ready"], 6)
                            act.activation(vst[:].rearrange("p i h w -> p (i h) w")[:, :, 0:HD],
                                           ps_m.rearrange("p (n d) -> p n d", d=HD), ACT.Copy).then_inc(drained["v"], 1)
                        if item == "on":
                            act.wait_ge(filled["on"], ob + 1)
                            if isinstance(ob, int) and ob == 0:
                                act.wait_ge(S["weights_loaded"], 16 * 7)
                            act.activation(onT_sb[:], ps_m, ACT.Identity, bias=bv_sb[:, 0:1]).then_inc(drained["on"], 1)
                        if item == "x1t":
                            act.wait_ge(S["x1_ready"], NQ * (ob + 1))
                            act.activation(x1[1][:, :, 0:D], x1[0][:, :, 0:D], ACT.Copy).then_inc(S["x1b_ready"], 1)
                            act.wait_ge(filled["x1t"], ob + 1)
                            act.activation(x1T_sb[:], ps_m, ACT.Copy).then_inc(drained["x1t"], 1)

            batches(act, body)
            pad_rows(act, mybir.EngineType.Activation, E // 2, E)
            act.wait_ge(S["top_link"], 15 * B)
            act.activation(lgm[:], lgm[:], ACT.Exp).then_inc(S["gate_exp"], 1)
            act.activation(dm[:], dm[:], ACT.Exp).then_inc(S["gate_exp"], 1)

            def step(i, r, found):
                j, u, _ = lagged(i, r, 0)
                if tile_live(j):
                    act.wait_ge(S["xsT_filled"], j + 1)
                    if not (isinstance(j, int) and j < 2):
                        act.wait_ge(S["h_filled"], j - 1)
                    act.activation(xsT[:, u % 2, :], psum[:, u % 2, 0:P], ACT.Copy).then_inc(S["xsT_copied"], 1)
                j, u, _ = lagged(i, r, 1)
                if tile_live(j):
                    act.wait_ge(S["h_filled"], j + 1)
                    if not (isinstance(j, int) and j < 2):
                        act.wait_ge(S["y_filled"], j - 1)
                    for ch in range(FC):
                        last = act.activation(hT_sb[:, u % 2, P * ch:P * ch + P], psum[:, 2 + u % 2, P * ch:P * ch + P],
                                              ACT.Gelu, bias=w_cur[:, u % WR, B1_AT + ch:B1_AT + ch + 1])
                    last.then_inc(S["gelu_done"], 1)

            expert_steps(act, step, LAG)

            def fin_step(i, r, _):
                q, u, _ = lagged(i, r, 0, FIN)
                if not (isinstance(q, int) and q < 2):
                    act.wait_ge(S["summed"], q - 1)
                for k in range(TOPK):
                    for n in range(NQ):
                        last = act.activation(diag[:, u % 2, k, n, :], ident[:], ACT.Copy,
                                              scale=gw[:, 4 + k, bass.ds(q * NQ + n, 1)])
                last.then_inc(S["diag_ready"], 1)

            act.wait_ge(S["gate_link"], 8)
            pipeline(act, fin_step, B, FIN, 0)

        @block.tensor
        def _(pe):
            def score_unit(b, c, u):
                n = (b * NG + c) * NUNIT + u
                if u == 0:
                    pe.wait_ge(qk_loaded[c], 80 * (b + 1))
                if not (isinstance(n, int) and n < 2):
                    pe.wait_ge(S["s_reduced"], n - 1)
                pair, kind = u // 3, u % 3
                for h in range(2):
                    g = 2 * pair + h
                    parts = {0: [(3, h, 0)], 1: [(2, h, 0), (0, h, 3 * P)], 2: [(1, 0, 2 * P * h)]}[kind]
                    for i, bank, at in parts:
                        w = P * (i + 1)
                        last_of_bank = kind < 2 or h == 1
                        pe.matmul(ps_s[:, u % 2, bank, at:at + w], qst[:, c, P * i:P * i + P], kst[:, c, g, 0:w],
                                  start=True, stop=False, skip_group_check=True)
                    if last_of_bank:
                        blocks = {0: ps_s[:, u % 2, h, 3 * P:T], 1: ps_s[:, u % 2, h, 2 * P:T],
                                  2: ps_s[:, u % 2, 0, :].rearrange("p (h w) -> p h w", h=2)[:, :, P:2 * P]}[kind]
                        mask = cmaskr[:, 0, :] if kind == 0 else cmaskr[:]
                        last = pe.matmul(blocks, identr[:], mask, start=False, stop=True, skip_group_check=True)
                last.then_inc(S["s_filled"], 1)

            def score_bank(b, c, k):
                n = (b * NG + c) * NBANK + k
                if k == 0:
                    pe.wait_ge(S["m_rows"], 16 * (b * NG + c + 1))
                if not (isinstance(n, int) and n < 2):
                    pe.wait_ge(S["exp_done"], n - 1)
                pair, kk = k // 5, k % 5
                for g in (2 * pair, 2 * pair + 1):
                    for j in range(NQ):
                        at, w = seg(g, j)
                        if at // T == kk:
                            last = pe.matmul(ps_t[:, k % 2, at % T:at % T + w], kst[:, c, g, P * j:P * j + P],
                                             qst[:, c, P * j:T], start=True, stop=True)
                last.then_inc(S["st_filled"], 1)

            def pv(b, c):
                n = b * NG + c
                pe.wait_ge(S["masked"], 6 * (n + 1))
                pe.wait_ge(drained["v"], b + 1)
                if not (isinstance(n, int) and n == 0):
                    pe.wait_ge(S["oT_copied"], n)
                for j in range(NQ):
                    for g in range(4):
                        at, w = seg(g, j)
                        last = pe.matmul(ps_o[32 * g:32 * g + 32, P * j:T], vst[:, j, 4 * g + c, :],
                                         probs[:, c % 2, g // 2, at:at + w], start=(j == 0), stop=(j == NQ - 1))
                last.then_inc(S["pv_filled"], 1)

            def shared(b, c, k, item):
                ob, oc, n = owner(b, c, item)
                if not live(ob):
                    return
                prev = before(b, c, k)
                if prev is not None:
                    pe.wait_ge(drained[prev[0]], prev[1])
                if item == "m":
                    pe.wait_ge(S["s_reduced"], NUNIT * (n + 1))
                    last = pe.transpose(ps_m[0:16, 0:P], nmax[:, oc, :], ident[:])
                if item == "ot":
                    pe.wait_ge(S["oT_copied"], n + 1)
                    for i in range(NQ):
                        last = pe.transpose(ps_m[:, P * i:P * i + P], oT_sb[:, P * i:P * i + P], ident[:])
                if item in ("q", "k"):
                    if isinstance(ob, int) and ob == 0:
                        pe.wait_ge(S["const_loaded"], 64)
                    pe.wait_ge(S["xT_loaded"], 16 * (ob + 1))
                    last = pe.matmul(ps_m, (wq_sb if item == "q" else wk_sb)[:], xT_sb[:], start=True, stop=True)
                if item == "v":
                    if isinstance(ob, int) and ob == 0:
                        pe.wait_ge(S["weights_loaded"], 16 * 7)
                    pe.wait_ge(S["xTv_loaded"], 16 * (ob + 1))
                    for i in range(NQ):
                        last = pe.matmul(ps_m[:, P * i:P * i + P], xTv_sb[:, P * i:P * i + P], wv_sb[:],
                                         start=True, stop=True)
                if item == "on":
                    pe.wait_ge(drained["ot"], NG * (ob + 1))
                    for i in range(NQ):
                        last = pe.transpose(ps_m[:, P * i:P * i + P], o_sb[:, P * i:P * i + P], ident[:])
                if item == "wo":
                    pe.wait_ge(drained["on"], ob + 1)
                    for i in range(NQ):
                        last = pe.matmul(ps_m[:, P * i:P * i + P], onT_sb[:, P * i:P * i + P], wo_sb[:],
                                         start=True, stop=True)
                if item == "x1t":
                    pe.wait_ge(S["x1_ready"], NQ * (ob + 1))
                    for i in range(NQ):
                        last = pe.transpose(ps_m[:, P * i:P * i + P], x1[0][:, i, 0:D], ident[:])
                if item == "lg":
                    pe.wait_ge(drained["x1t"], ob + 1)
                    for i in range(NQ):
                        last = pe.matmul(ps_m[:, E * i:E * i + E], x1T_sb[:, P * i:P * i + P], gate_sb[:],
                                         start=True, stop=True)
                if item == "rk":
                    pe.wait_ge(S["hot_ready"], ob + 1)
                    pe.matmul(ps_m[:, 0:EB], tri[:], hotb[:].rearrange("p i e -> p (i e)"), start=True, stop=False,
                              skip_group_check=True)
                    for i in range(NQ):
                        for o in range(i + 1, NQ):
                            pe.matmul(ps_m[:, E * o:E * o + E], ones[:], hotb[:, i, :], start=False, stop=False,
                                      skip_group_check=True)
                        last = pe.matmul(ps_m[:, EB:EB + E], ones[:], hotb[:, i, :], start=False, stop=(i == NQ - 1),
                                         skip_group_check=True)
                last.then_inc(filled[item], 1)

            def body(b):
                for c in range(NG):
                    sb_, sc_ = ahead(b, c, 2)
                    pb_, pc_ = ahead(b, c, -1)
                    if isinstance(b, int) and b == -1 and c == 2:
                        pe.wait_ge(S["idents_ready"], 2)
                        pe.wait_ge(S["masks_ready"], 4)
                        pe.wait_ge(S["const_ready"], 6)
                    for k in range(NBANK):
                        if live(b):
                            score_bank(b, c, k)
                        if k in UNIT_AT and live(sb_):
                            score_unit(sb_, sc_, UNIT_AT[k])
                        if k == PV_AT and live(pb_):
                            pv(pb_, pc_)
                        if (c, k) in MISC:
                            shared(b, c, k, MISC[(c, k)])

            batches(pe, body)
            pe.wait_ge(drained["rk"], B)
            pe.wait_ge(S["tab_link"], TAB_STEPS)
            pe.transpose(ps_m[0:2, 0:P], tile_tab[:], ident[:]).then_inc(S["tab_T"], 1)
            pe.wait_ge(S["experts_loaded"], 16 * 3)
            pe.wait_ge(S["tables_ready"], 1)

            def step(i, r, found):
                j, u, ii = lagged(i, r, 0)
                if tile_live(j):
                    pe.wait_ge(xs_loaded[r], 16 * (ii + 1))
                    if not (isinstance(j, int) and j < 2):
                        pe.wait_ge(S["xsT_copied"], j - 1)
                    pe.transpose(psum[:, r % 2, 0:P], xs[:, r, 0:D], ident[:]).then_inc(S["xsT_filled"], 1)
                j, u, ii = lagged(i, r, 1)
                if tile_live(j):
                    pe.wait_ge(S["xsT_copied"], j + 1)
                    pe.wait_ge(S["w_copied"], j + 1)
                    if not (isinstance(j, int) and j < 2):
                        pe.wait_ge(S["gelu_done"], j - 1)
                    for ch in range(FC):
                        last = pe.matmul(psum[:, 2 + u % 2, P * ch:P * ch + P], w_cur[:, u % WR, P * ch:P * ch + P],
                                         xsT[:, u % 2, :], start=True, stop=True)
                    last.then_inc(S["h_filled"], 1)
                j, u, ii = lagged(i, r, 2)
                if tile_live(j):
                    pe.wait_ge(S["gelu_done"], j + 1)
                    if not (isinstance(j, int) and j < 4):
                        pe.wait_ge(S["y_copied"], j - 3)
                    for ch in range(FC):
                        last = pe.matmul(psum[:, 4 + u % 4, 0:D], hT_sb[:, u % 2, P * ch:P * ch + P],
                                         w_cur[:, u % WR, W2_AT + P * ch:W2_AT + P * ch + D],
                                         start=(ch == 0), stop=(ch == FC - 1))
                    last.then_inc(S["y_filled"], 1)

            expert_steps(pe, step, LAG)

            def fin_step(i, r, _):
                q, u, ii = lagged(i, r, 0, FIN)
                pe.wait_ge(S["diag_ready"], q + 1)
                pe.wait_ge(o_loaded[u], 32 * (ii + 1))
                if not (isinstance(q, int) and q < 2):
                    pe.wait_ge(S["clipped"], q - 1)
                for n in range(NQ):
                    sums = psum[:, u % 2, P * n:P * n + P]
                    pe.matmul(sums, ident[:], xr[:, bass.ds(q * T + P * n, P)], start=True, stop=False)
                    for k in range(TOPK):
                        last = pe.matmul(sums, diag[:, u % 2, k, n, :], fin[:, u, k, P * n:P * n + P],
                                         start=False, stop=(k == TOPK - 1))
                last.then_inc(S["summed"], 1)

            pipeline(pe, fin_step, B, FIN, 0)

        @block.vector
        def _(dve):
            def linker(s, base):
                n = [0]

                def link(ins):
                    n[0] += 1
                    ins.then_inc(s, 1)
                    dve.wait_ge(s, base + n[0])
                return link

            dve.memset(probs[0:H, 0, 0, 0:T], 0.0).then_inc(S["scratch_src"], 1)
            dve.memset(probs[0:H, 1, 0, 0:T], 1.0).then_inc(S["scratch_src"], 1)

            def reduce_unit(b, c, u):
                n = (b * NG + c) * NUNIT + u
                dve.wait_ge(S["s_filled"], n + 1)
                pair, kind = u // 3, u % 3
                ps = ps_s[:, u % 2]
                mx = nmax[:, c, :].rearrange("p (g i) -> p g i", g=4)[:, 2 * pair:2 * pair + 2, :]
                if kind == 0:
                    todo = [(mx[:, :, 3], ps[:, :, :])]
                elif kind == 1:
                    todo = [(mx[:, :, 2], ps[:, :, 0:3 * P]), (mx[:, :, 0], ps[:, :, 3 * P:T])]
                else:
                    todo = [(mx[:, :, 1], ps[:, 0, :].rearrange("p (h w) -> p h w", h=2))]
                for o, i in todo:
                    last = dve.tensor_reduce(o, i, AX.X, ALU.max, negate=True)
                last.then_inc(S["s_reduced"], 1)

            def shared(b, c, item):
                ob, oc, n = owner(b, c, item)
                if not live(ob):
                    return
                first = isinstance(ob, int) and ob == 0
                done = drained[item]
                if item in ("q", "k"):
                    dve.wait_ge(S[item + "_hi_done"], ob + 1)
                    bias = bq_sb if item == "q" else bk_sb
                    if not first:
                        dve.wait_ge(S["qk_stored"], ob * 96)
                    dve.scalar_tensor_tensor(out=nat[item + "_lo"][:], in0=ps_m, scalar=bias[:, 0:1],
                                             in1=nat[item + "_hi"][:].bitcast(F32), op0=ALU.add,
                                             op1=ALU.subtract).then_inc(done, 1)
                if item == "ot":
                    dve.wait_ge(filled["ot"], n + 1)
                    if oc == 0 and not first:
                        dve.wait_ge(filled["on"], ob)
                    pv = ps_m.rearrange("p (n w) -> p n w", w=32)
                    dve.reciprocal(rz[:].unsqueeze(2), pv[:, :, HD:HD + 1]).then_inc(S["rz_ready"], 1)
                    dve.wait_ge(S["rz_ready"], n + 1)
                    o = o_sb[:].rearrange("p (n c d) -> p n c d", c=NG, d=HD)[:, :, oc, :]
                    dve.tensor_tensor(o, pv[:, :, 0:HD], rz[:].unsqueeze(2).to_broadcast([P, NQ * 4, HD]),
                                      ALU.mult).then_inc(done, 1)
                if item == "wo":
                    dve.wait_ge(filled["wo"], ob + 1)
                    dve.wait_ge(S["xbo_ready"], ob + 1)
                    dve.tensor_tensor(y[:].rearrange("p i d -> p (i d)"), ps_m,
                                      xbo[:].rearrange("p i d -> p (i d)"), ALU.add).then_inc(done, 1)
                    dve.wait_ge(done, ob + 1)
                    for i in range(NQ):
                        dve.bn_stats(st[:, i, :], y[:, i, :]).then_inc(S["stats_ready"], 1)
                    for i in range(NQ):
                        dve.wait_ge(S["stats_ready"], NQ * ob + i + 1)
                        dve.sem_inc(S["dve_turn"], 1)
                        dve.bn_aggr(mv[:, i, :], st[:, i, :]).then_inc(S["aggr_ready"], 1)
                if item == "lg":
                    dve.wait_ge(filled["lg"], ob + 1)
                    dve.tensor_copy(lg[:].rearrange("p i e -> p (i e)"), ps_m[:, 0:EB]).then_inc(done, 1)
                if item == "rk":
                    dve.wait_ge(filled["rk"], ob + 1)
                    dve.wait_ge(S["top_link"], 15 * (ob + 1))
                    dve.tensor_tensor(rank[:], ps_m[:, 0:EB].rearrange("p (i e) -> p i e", i=NQ),
                                      nxt[:].unsqueeze(1).to_broadcast([P, NQ, E]), ALU.add
                                      ).then_inc(S["rank_link"], 1)
                    dve.wait_ge(S["rank_link"], 5 * ob + 1)
                    dve.tensor_tensor(nxt[:], nxt[:], ps_m[:, EB:EB + E], ALU.add).then_inc(done, 1)

            def bc(a):
                return a.unsqueeze(2).to_broadcast([P, NQ, E])

            def top_wait(b, n):
                dve.wait_ge(S["top_link"], 15 * b + n)

            def top_part(b, part):
                link = S["top_link"]
                if part in (0, 3):
                    k, cur, n = (0, lg, 0) if part == 0 else (1, lg2, 6)
                    if part == 0:
                        dve.wait_ge(drained["lg"], b + 1)
                    else:
                        top_wait(b, n)
                    dve.tensor_reduce(top[:, 2 * k, :], cur[:], AX.X, ALU.max).then_inc(link, 1)
                    top_wait(b, n + 1)
                    dve.tensor_tensor(tmp[:], cur[:], bc(top[:, 2 * k, :]), ALU.is_equal).then_inc(link, 1)
                if part in (1, 4):
                    k, n = (0, 2) if part == 1 else (1, 8)
                    top_wait(b, n)
                    dve.tensor_tensor(tm1[:], tmp[:], rev[:], ALU.mult).then_inc(link, 1)
                    top_wait(b, n + 1)
                    dve.tensor_reduce(top[:, 2 * k + 1, :], tm1[:], AX.X, ALU.max).then_inc(link, 1)
                if part == 2:
                    top_wait(b, 4)
                    dve.tensor_tensor(hot[0][:], rev[:], bc(top[:, 1, :]), ALU.is_equal).then_inc(link, 1)
                    top_wait(b, 5)
                    dve.scalar_tensor_tensor(out=lg2[:], in0=hot[0][:], scalar=-3e38, in1=lg[:], op0=ALU.mult,
                                             op1=ALU.add).then_inc(link, 1)
                if part == 5:
                    top_wait(b, 10)
                    dve.tensor_tensor(hot[1][:], rev[:], bc(top[:, 3, :]), ALU.is_equal).then_inc(link, 1)
                    top_wait(b, 11)
                    dve.tensor_tensor(hotb[:], hot[0][:], hot[1][:], ALU.add).then_inc(S["hot_ready"], 1)
                if part == 6:
                    dve.tensor_tensor(lgm[:, bass.ds(b * EB, EB)].rearrange("p (i e) -> p i e", i=NQ), lg[:],
                                      bc(top[:, 0, :]), ALU.subtract).then_inc(link, 1)
                    dve.tensor_tensor(dm[:, bass.ds(b * NQ, NQ)], top[:, 2, :], top[:, 0, :], ALU.subtract
                                      ).then_inc(link, 1)
                    if not (isinstance(b, int) and b == 0):
                        dve.wait_ge(S["top_link"], 15 * b)
                    dve.tensor_copy(x1[0][:, :, D:D + 1].bitcast(I32), slot[:, 0, :].unsqueeze(2)).then_inc(link, 1)
                    dve.tensor_copy(x1[1][:, :, D:D + 1].bitcast(I32), slot[:, 1, :].unsqueeze(2)
                                    ).then_inc(S["x1_ids"], 1)
                    dve.wait_ge(S["x1_ids"], b + 1)
                    dve.tensor_scalar(slot[:], slot[:], float(T), None, ALU.add).then_inc(link, 1)

            def rank_part(b, part):
                link = S["rank_link"]
                if part == 0:
                    for k, t in ((0, tmp), (1, tm1)):
                        dve.tensor_tensor(t[:], hot[k][:], rank[:], ALU.mult).then_inc(link, 1)
                if part == 1:
                    for k, t in ((0, tmp), (1, tm1)):
                        dve.wait_ge(link, 5 * b + 2 + k)
                        dve.tensor_reduce(posf[:, k, :], t[:], AX.X, ALU.add).then_inc(link, 1)
                if part == 2:
                    dve.wait_ge(link, 5 * (b + 1))
                    if not (isinstance(b, int) and b == 0):
                        dve.wait_ge(S["scattered"], b * NQ * TOPK * 16)
                    dve.tensor_copy(pos[:], posf[:]).then_inc(S["pos_ready"], 1)

            def layernorm_rows(b):
                if not (isinstance(b, int) and b == 0):
                    dve.wait_ge(S["scattered"], b * NQ * TOPK * 16)
                    dve.wait_ge(S["xr_copied"], 16 * b)
                dve.wait_ge(S["rstd_ready"], b + 1)
                for i in range(NQ):
                    dve.tensor_scalar(x1[0][:, i, 0:D], y[:, i, :], mv[:, i, 0:1], rstd[:, i:i + 1],
                                      ALU.subtract, ALU.mult).then_inc(S["x1_ready"], 1)

            def body(b):
                for c in range(NG):
                    if isinstance(b, int) and b == -1 and c == 1:
                        dve.memset(ones[:], 1.0).then_inc(S["const_ready"], 1)
                        dve.memset(vst[:, :, :, HD + 1:32], 0.0).then_inc(S["const_ready"], 1)
                        dve.memset(vst[:, :, :, HD:HD + 1], 1.0).then_inc(S["const_ready"], 1)
                        dve.memset(x1[0][:, :, D:ROW], 0.0)
                        dve.memset(x1[1][:, :, D:ROW], 0.0)
                        dve.wait_ge(S["idents_ready"], 2)
                        dve.tensor_copy(identr[:], ident[:]).then_inc(S["const_ready"], 1)
                        dve.wait_ge(S["masks_ready"], 4)
                        dve.tensor_copy(cmaskr[:], cmask[:].unsqueeze(1).to_broadcast([P, 2, P])
                                        ).then_inc(S["const_ready"], 1)
                    if isinstance(b, int) and b == B - 2 and c == 1:
                        dve.wait_ge(S["weights_loaded"], 16 * 7)
                        dve.tensor_copy(experts[:, :, B1_AT:W2_AT], b1_sb[:]).then_inc(S["bias_placed"], 1)
                    sb_, sc_ = ahead(b, c, 2)
                    for k in range(NBANK):
                        if k in UNIT_AT and live(sb_):
                            reduce_unit(sb_, sc_, UNIT_AT[k])
                        if (c, k) in MISC:
                            shared(b, c, MISC[(c, k)])
                        if (c, k) == LN_AT and live(b - 1):
                            layernorm_rows(b - 1)
                        if (c, k) in TOP_AT and live(b - 1):
                            for part in TOP_AT[c, k]:
                                top_part(b - 1, part)
                        if (c, k) in RANK_AT and live(b - 1):
                            for part in RANK_AT[c, k]:
                                rank_part(b - 1, part)

            batches(dve, body)

            dve.wait_ge(S["iota_ready"], 7)
            dve.wait_ge(drained["rk"], B)
            tab = linker(S["tab_link"], 0)
            rows_of, tiles_of, upto, step_to = (tabs[:, n, :] for n in range(4))
            tab(dve.tensor_copy(first_free[:], nxt[0:1, :]))
            tab(dve.tensor_tensor(rows_of, nxt[:], reg0[:], ALU.subtract))
            tab(dve.tensor_scalar(rows_of, rows_of, 1.0 / P, (P - 1.0) / P - 0.5 + 1.0 / 512, ALU.mult, ALU.add))
            tab(dve.tensor_copy(tabs_i[:], rows_of))
            tab(dve.tensor_copy(tiles_of, tabs_i[:]))
            tab(dve.memset(rows_of, 1.0))
            tab(dve.tensor_tensor_scan(upto, rows_of, tiles_of, 0.0, ALU.mult, ALU.add))
            tab(dve.tensor_scalar(step_to, tiles_of, -float(P), float(REG), ALU.mult, ALU.add))
            passed, moved = tabs[:, 0, :], tabs[:, 1, :]
            tab(dve.tensor_scalar(passed, upto, tile_no[:, 0:1], None, ALU.is_le))
            tab(dve.tensor_tensor(moved, passed, step_to, ALU.mult))
            tab(dve.tensor_reduce(tile_tab[:], tabs[:, 0:2, :], AX.X, ALU.add))
            tab(dve.scalar_tensor_tensor(out=tile_tab[:, 1:2], in0=tile_no[:], scalar=float(P), in1=tile_tab[:, 1:2],
                                         op0=ALU.mult, op1=ALU.add))
            tab(dve.tensor_scalar(tile_tab[:, 0:1], tile_tab[:, 0:1], float(E - 1), float(WCOLS), ALU.min, ALU.mult))
            tab(dve.tensor_scalar(tile_tab[:, 1:2], tile_tab[:, 1:2], float(DUMP), None, ALU.min))
            dve.wait_ge(S["tab_T"], 1)
            dve.tensor_copy(tile_ei[:], ps_m[0:2, 0:P]).then_inc(S["tables_ready"], 1)
            dve.wait_ge(S["tables_ready"], 1)
            dve.wait_ge(S["bias_placed"], 1)
            dve.wait_ge(S["experts_loaded"], 16 * 3)

            def step(i, r, found):
                j, u, _ = lagged(i, r, WR)
                if tile_live(j):
                    dve.wait_ge(S["y_filled"], j + 1)
                    dve.tensor_tensor(y_sb[:, u, :], psum[:, 4 + u % 4, 0:D], w_cur[:, u % WR, B2_AT:WCOLS],
                                      ALU.add).then_inc(S["y_copied"], 1)
                j, u, _ = lagged(i, r, 0)
                if tile_live(j):
                    if not (isinstance(j, int) and j < WR):
                        dve.wait_ge(S["y_copied"], j - WR + 1)
                    dve.tensor_copy(w_cur[:, u % WR, :],
                                    experts[:].rearrange("p e f -> p (e f)")[:, bass.ds(found, WCOLS)]
                                    ).then_inc(S["w_copied"], 1)

            expert_steps(dve, step, WR, (mybir.EngineType.DVE, 0, (E - 1) * WCOLS))

            dve.wait_ge(S["gate_exp"], 2)
            gate = linker(S["gate_link"], 0)
            g = lambda n: gw[:, n, :]
            gate(dve.tensor_reduce(g(0), lgm[:].rearrange("p (t e) -> p t e", e=E), AX.X, ALU.add))
            gate(dve.reciprocal(g(1), g(0)))
            gate(dve.tensor_tensor(g(2), dm[:], g(1), ALU.mult))
            gate(dve.tensor_tensor(g(0), g(1), g(2), ALU.add))
            gate(dve.tensor_scalar(g(0), g(0), 1e-10, None, ALU.max))
            gate(dve.reciprocal(g(3), g(0)))
            gate(dve.tensor_tensor(g(4), g(1), g(3), ALU.mult))
            gate(dve.tensor_tensor(g(5), g(2), g(3), ALU.mult))

            def fin_step(i, r, _):
                q, u, ii = lagged(i, r, 0, FIN)
                if tile_live(q, B):
                    dve.wait_ge(S["summed"], q + 1)
                    if not (isinstance(q, int) and q < FIN):
                        dve.wait_ge(out_stored[u], 16 * ii)
                    dve.tensor_scalar(fin[:, u, 2, :], psum[:, u % 2, :], 100.0, -100.0, ALU.min, ALU.max
                                      ).then_inc(S["clipped"], 1)
                q, u, _ = lagged(i, r, 1, FIN)
                if tile_live(q, B):
                    dve.wait_ge(S["residual_added"], q + 1)
                    if not (isinstance(q, int) and q < 2):
                        dve.wait_ge(S["fin_aggr"], NQ * (q - 1))
                    for n in range(NQ):
                        dve.bn_stats(fin_st[:, u % 2, n, :], fin[:, u, 2, P * n:P * n + P]).then_inc(S["fin_stats"], 1)
                    if not (isinstance(q, int) and q < 2):
                        dve.wait_ge(S["fin_ready"], q - 1)
                        dve.sem_inc(S["dve_turn"], 1)
                    for n in range(NQ):
                        dve.wait_ge(S["fin_stats"], NQ * q + n + 1)
                        dve.sem_inc(S["dve_turn"], 1)
                        dve.bn_aggr(fin_mv[:, u % 2, n, :], fin_st[:, u % 2, n, :]).then_inc(S["fin_aggr"], 1)
                q, u, _ = lagged(i, r, 2, FIN)
                if tile_live(q, B):
                    dve.wait_ge(S["fin_rstd"], q + 1)
                    for n in range(NQ):
                        rows = fin[:, u, 2, P * n:P * n + P]
                        last = dve.tensor_scalar(rows, rows, fin_mv[:, u % 2, n, 0:1], fin_rs[:, u % 2, n:n + 1],
                                                 ALU.subtract, ALU.mult)
                    last.then_inc(S["fin_ready"], 1)

            pipeline(dve, fin_step, B, FIN, FIN_LAG)


_NAMES = ['x', 'xT', 'WqT', 'bq', 'WkT', 'bk', 'WvT', 'bv', 'WoT', 'bo', 'gateT', 'w1', 'b1T', 'w2', 'b2']


def kernel(**inputs):
    import numpy as _np
    import concourse.bacc as _bacc
    from concourse import mybir as _mybir
    from concourse.bass_utils import run_bass_kernel_spmd as _run

    a = {k: _np.asarray(v) for k, v in inputs.items()}
    laid = {
        'x': a['L0_attn_x'], 'xT': a['L0_attn_x'].transpose(0, 2, 1),
        'WqT': a['L0_attn_Wq'].T, 'bq': a['L0_attn_bq'].reshape(-1, 1),
        'WkT': a['L0_attn_Wk'].T, 'bk': a['L0_attn_bk'].reshape(-1, 1),
        'WvT': a['L0_attn_Wv'].T, 'bv': a['L0_attn_bv'].reshape(-1, 1),
        'WoT': a['L0_attn_Wo'].T, 'bo': a['L0_attn_bo'].reshape(1, -1),
        'gateT': a['L0_ffn_gate_w'].T, 'w1': a['L0_ffn_w1'], 
        'b1T': a['L0_ffn_b1'].reshape(a['L0_ffn_b1'].shape[0], -1, 128).transpose(2, 0, 1),
        'w2': a['L0_ffn_w2'], 'b2': a['L0_ffn_b2'].reshape(1, -1),
    }
    nc = _bacc.Bacc("TRN2", target_bir_lowering=False, num_devices=1)
    arrays, args = {}, []
    for name in _NAMES:
        v = _np.ascontiguousarray(laid[name])
        arrays[f"in_{name}"] = v
        args.append(nc.dram_tensor(f"in_{name}", v.shape, _mybir.dt.from_np(v.dtype), kind="ExternalInput").ap())
    out = nc.dram_tensor("out", laid['x'].shape, F32, kind="ExternalOutput").ap()
    post_ln_attention_moe(nc, *args, out)
    r = _run(nc, [arrays], core_ids=[0])
    return r.results[0]["out"]
```
